# Optimizing a Trainium2 kernel written in Bass

```python
import numpy as np
import jax
import jax.numpy as jnp

def _softmax(x, axis=-1):
    return jax.nn.softmax(x, axis=axis)

def _gelu(x):
    return jax.nn.gelu(x, approximate=True)

def _silu(x):
    return jax.nn.silu(x)

def _sigmoid(x):
    return jax.nn.sigmoid(x)

def _layernorm(x, axis=-1, eps=1e-05):
    m = jnp.mean(x, axis=axis, keepdims=True)
    v = jnp.var(x, axis=axis, keepdims=True)
    return (x - m) / jnp.sqrt(v + eps)

def _scatter_add(tgt, idx, src, axis=0):
    return tgt.at[idx].add(src)

def _segment_sum(src, seg, n):
    return jax.ops.segment_sum(src, seg, n)
kernel_name = 'mk_xattn_seq_d2_seqx_r4_d8e294'

def setup_inputs(seed: int=0):
    np.random.seed(seed)
    _w = jnp.asarray

    def _rec_inputs():
        import jax
        import jax.numpy as jnp
        _rk = jax.random.key(seed)
        x = -0.0003929 + 0.9999 * jax.random.normal(jax.random.fold_in(_rk, 1), (8, 256, 512), jnp.float32)
        _lenS = 256 - jax.random.randint(jax.random.fold_in(_rk, 7), (8,), 0, max(1, 256 // 4) + 1, jnp.int32)
        _lenS2 = 256 - jax.random.randint(jax.random.fold_in(_rk, 8), (8,), 0, max(1, 256 // 4) + 1, jnp.int32)
        _ctx_2048P = jax.random.normal(jax.random.fold_in(_rk, 11), (8, 16, 512), jnp.float32)
        _ctx_2048c = jax.random.dirichlet(jax.random.fold_in(_rk, 511), 0.3 * jnp.ones((16,), jnp.float32), (8, 256))
        _ctx_2048t = jnp.einsum('bsk,bkd->bsd', _ctx_2048c, _ctx_2048P)
        _ctx_2048t = _ctx_2048t * jax.lax.rsqrt(jnp.mean(jnp.square(_ctx_2048t)) + 1e-12) * 0.953939
        ctx_2048 = 2.81802e-05 + 1.00001 * (_ctx_2048t + 0.3 * jax.random.normal(jax.random.fold_in(_rk, 611), (8, 256, 512), jnp.float32))
        return (x, ctx_2048)
    x, ctx_2048 = _rec_inputs()

    def _L0_xattn_setup():
        import jax, jax.numpy as jnp
        import numpy as np
        B, C1, C2, N = (8, 256, 256, 512)
        D = C2 // 8
        key = jax.random.key(seed)
        ks = jax.random.split(key, 8)
        s1 = 1.0 / np.sqrt(C1)
        s2 = 1.0 / np.sqrt(C2)
        return {'x1': jax.random.normal(ks[0], (B, C1, N), jnp.float32), 'x2': jax.random.normal(ks[1], (B, C2, N), jnp.float32), 'Wq': jax.random.uniform(ks[2], (D, C1), jnp.float32, -s1, s1), 'bq': jax.random.uniform(ks[3], (D,), jnp.float32, -s1, s1), 'Wk': jax.random.uniform(ks[4], (D, C2), jnp.float32, -s2, s2), 'bk': jax.random.uniform(ks[5], (D,), jnp.float32, -s2, s2), 'Wv': jax.random.uniform(ks[6], (C1, C2), jnp.float32, -s2, s2), 'bv': jax.random.uniform(ks[7], (C1,), jnp.float32, -s2, s2)}
    _L0_xattn_all = _L0_xattn_setup()
    _L0_xattn_in = {k: v for k, v in _L0_xattn_all.items() if k in ('Wq', 'bq', 'Wk', 'bk', 'Wv', 'bv')}
    del _L0_xattn_all

    def _L1_xattn_setup():
        import jax, jax.numpy as jnp
        import numpy as np
        E, H, L, B = (512, 32, 256, 4)
        S = E // H
        DM, DD = (32, 64)

        def _ln(x, w, b, eps=1e-05):
            m = x.mean(-1, keepdims=True)
            v = ((x - m) ** 2).mean(-1, keepdims=True)
            return (x - m) / jnp.sqrt(v + eps) * w + b

        def _block(x, state, ln1_w, ln1_b, ln2_w, ln2_b, maa_x, maa_w1, maa_w2, maa_stack, time_decay, td_w1, td_w2, u, Wr, Wk, Wv, Wg, Wo, gn_w, gn_b, ffn_maa_k, ffn_maa_r, Wfk, Wfr, Wfv):
            b, l, e = x.shape
            h = u.shape[0]
            s_ = e // h
            xa = _ln(x, ln1_w, ln1_b)
            sx = jnp.concatenate([state[:, 1:2] - xa[:, :1], xa[:, :-1] - xa[:, 1:]], axis=1)
            xxx = jnp.tanh((xa + sx * maa_x) @ maa_w1).reshape(b, l, 5, DM)
            xxx = jnp.einsum('blfd,fde->blfe', xxx, maa_w2)
            xm = xa[:, :, None] + sx[:, :, None] * (maa_stack + xxx)
            xk, xw, xv, xr, xg = (xm[:, :, j] for j in range(5))
            w = jnp.exp(-jnp.exp(time_decay + jnp.tanh(xw @ td_w1) @ td_w2)).reshape(b, l, h, s_)
            r = (xr @ Wr.T).reshape(b, l, h, s_)
            k = (xk @ Wk.T).reshape(b, l, h, s_)
            v = (xv @ Wv.T).reshape(b, l, h, s_)
            g = jax.nn.silu(xg @ Wg.T)
            s0 = state[:, 2:2 + s_].reshape(b, h, s_, s_)

            def step(s, rkvw):
                r_t, k_t, v_t, w_t = rkvw
                a = k_t[..., :, None] * v_t[..., None, :]
                out = jnp.einsum('bhi,bhij->bhj', r_t, u * a + s)
                s = a + w_t[..., :, None] * s
                return (s, out)
            rkvw = tuple((jnp.moveaxis(t, 1, 0) for t in (r, k, v, w)))
            _, out = jax.lax.scan(step, s0, rkvw)
            out = jnp.moveaxis(out, 0, 1).reshape(b, l, e)
            og = out.reshape(b, l, h, s_)
            m = og.mean(-1, keepdims=True)
            va = ((og - m) ** 2).mean(-1, keepdims=True)
            og = ((og - m) / jnp.sqrt(va + 1e-05)).reshape(b, l, e) * gn_w + gn_b
            x1 = x + og * g @ Wo.T
            xc = _ln(x1, ln2_w, ln2_b)
            sx2 = jnp.concatenate([state[:, 0:1] - xc[:, :1], xc[:, :-1] - xc[:, 1:]], axis=1)
            xk2 = xc + sx2 * ffn_maa_k
            xr2 = xc + sx2 * ffn_maa_r
            rr = jax.nn.sigmoid(xr2 @ Wfr.T)
            kk = jnp.square(jax.nn.relu(xk2 @ Wfk.T))
            return x1 + rr * (kk @ Wfv.T)
        key = jax.random.key(seed)
        ks = jax.random.split(key, 24)
        sc = 0.02
        d = {'x': jax.random.normal(ks[0], (B, L, E), jnp.float32), 'state': jax.random.normal(ks[1], (B, 2 + S, E), jnp.float32) * 0.1, 'ln1_w': jnp.ones((E,), jnp.float32), 'ln1_b': jnp.zeros((E,), jnp.float32), 'ln2_w': jnp.ones((E,), jnp.float32), 'ln2_b': jnp.zeros((E,), jnp.float32), 'maa_x': jax.random.normal(ks[2], (E,), jnp.float32) * 0.1, 'maa_w1': jax.random.normal(ks[3], (E, 5 * DM), jnp.float32) * sc, 'maa_w2': jax.random.normal(ks[4], (5, DM, E), jnp.float32) * sc, 'maa_stack': jax.random.normal(ks[5], (1, 5, E), jnp.float32) * 0.1, 'time_decay': jax.random.normal(ks[6], (E,), jnp.float32) * 0.5, 'td_w1': jax.random.normal(ks[7], (E, DD), jnp.float32) * sc, 'td_w2': jax.random.normal(ks[8], (DD, E), jnp.float32) * sc, 'u': jax.random.normal(ks[9], (H, S, 1), jnp.float32) * 0.1, 'Wr': jax.random.normal(ks[10], (E, E), jnp.float32) * sc, 'Wk': jax.random.normal(ks[11], (E, E), jnp.float32) * sc, 'Wv': jax.random.normal(ks[12], (E, E), jnp.float32) * sc, 'Wg': jax.random.normal(ks[13], (E, E), jnp.float32) * sc, 'Wo': jax.random.normal(ks[14], (E, E), jnp.float32) * sc, 'gn_w': jnp.ones((E,), jnp.float32), 'gn_b': jnp.zeros((E,), jnp.float32), 'ffn_maa_k': jax.random.normal(ks[15], (E,), jnp.float32) * 0.1, 'ffn_maa_r': jax.random.normal(ks[16], (E,), jnp.float32) * 0.1, 'Wfk': jax.random.normal(ks[17], (E, E), jnp.float32) * sc, 'Wfr': jax.random.normal(ks[18], (E, E), jnp.float32) * sc, 'Wfv': jax.random.normal(ks[19], (E, E), jnp.float32) * sc}
        return d
    _L1_xattn_all = _L1_xattn_setup()
    _L1_xattn_in = {k: v for k, v in _L1_xattn_all.items() if k in ('ln1_w', 'ln1_b', 'ln2_w', 'ln2_b', 'maa_x', 'maa_w1', 'maa_w2', 'maa_stack', 'time_decay', 'td_w1', 'td_w2', 'u', 'Wr', 'Wk', 'Wv', 'Wg', 'Wo', 'gn_w', 'gn_b', 'ffn_maa_k', 'ffn_maa_r', 'Wfk', 'Wfr', 'Wfv')}
    del _L1_xattn_all
    return {'x': x, 'ctx_2048': ctx_2048, 'L0_xattn_Wq': _L0_xattn_in['Wq'], 'L0_xattn_bq': _L0_xattn_in['bq'], 'L0_xattn_Wk': _L0_xattn_in['Wk'], 'L0_xattn_bk': _L0_xattn_in['bk'], 'L0_xattn_Wv': _L0_xattn_in['Wv'], 'L0_xattn_bv': _L0_xattn_in['bv'], 'L1_xattn_ln1_w': _L1_xattn_in['ln1_w'], 'L1_xattn_ln1_b': _L1_xattn_in['ln1_b'], 'L1_xattn_ln2_w': _L1_xattn_in['ln2_w'], 'L1_xattn_ln2_b': _L1_xattn_in['ln2_b'], 'L1_xattn_maa_x': _L1_xattn_in['maa_x'], 'L1_xattn_maa_w1': _L1_xattn_in['maa_w1'], 'L1_xattn_maa_w2': _L1_xattn_in['maa_w2'], 'L1_xattn_maa_stack': _L1_xattn_in['maa_stack'], 'L1_xattn_time_decay': _L1_xattn_in['time_decay'], 'L1_xattn_td_w1': _L1_xattn_in['td_w1'], 'L1_xattn_td_w2': _L1_xattn_in['td_w2'], 'L1_xattn_u': _L1_xattn_in['u'], 'L1_xattn_Wr': _L1_xattn_in['Wr'], 'L1_xattn_Wk': _L1_xattn_in['Wk'], 'L1_xattn_Wv': _L1_xattn_in['Wv'], 'L1_xattn_Wg': _L1_xattn_in['Wg'], 'L1_xattn_Wo': _L1_xattn_in['Wo'], 'L1_xattn_gn_w': _L1_xattn_in['gn_w'], 'L1_xattn_gn_b': _L1_xattn_in['gn_b'], 'L1_xattn_ffn_maa_k': _L1_xattn_in['ffn_maa_k'], 'L1_xattn_ffn_maa_r': _L1_xattn_in['ffn_maa_r'], 'L1_xattn_Wfk': _L1_xattn_in['Wfk'], 'L1_xattn_Wfr': _L1_xattn_in['Wfr'], 'L1_xattn_Wfv': _L1_xattn_in['Wfv']}

def reference(x, ctx_2048, L0_xattn_Wq, L0_xattn_bq, L0_xattn_Wk, L0_xattn_bk, L0_xattn_Wv, L0_xattn_bv, L1_xattn_ln1_w, L1_xattn_ln1_b, L1_xattn_ln2_w, L1_xattn_ln2_b, L1_xattn_maa_x, L1_xattn_maa_w1, L1_xattn_maa_w2, L1_xattn_maa_stack, L1_xattn_time_decay, L1_xattn_td_w1, L1_xattn_td_w2, L1_xattn_u, L1_xattn_Wr, L1_xattn_Wk, L1_xattn_Wv, L1_xattn_Wg, L1_xattn_Wo, L1_xattn_gn_w, L1_xattn_gn_b, L1_xattn_ffn_maa_k, L1_xattn_ffn_maa_r, L1_xattn_Wfk, L1_xattn_Wfr, L1_xattn_Wfv):
    import jax
    import jax.numpy as jnp

    def _L0_xattn_ref(x1, x2, Wq, bq, Wk, bk, Wv, bv):
        import jax, jax.numpy as jnp
        import numpy as np
        B, C1, C2, N = (8, 256, 256, 512)
        D = C2 // 8
        q = jnp.einsum('bcn,dc->bnd', x1, Wq) + bq
        k = jnp.einsum('bcn,dc->bdn', x2, Wk) + bk[:, None]
        v = jnp.einsum('bcn,dc->bdn', x2, Wv) + bv[:, None]
        attn = jax.nn.softmax(jnp.einsum('bnd,bdm->bnm', q, k), axis=2)
        attn_out = jnp.einsum('bcm,bnm->bcn', v, attn)
        return attn_out + x1

    def _L1_xattn_ref(x, state, ln1_w, ln1_b, ln2_w, ln2_b, maa_x, maa_w1, maa_w2, maa_stack, time_decay, td_w1, td_w2, u, Wr, Wk, Wv, Wg, Wo, gn_w, gn_b, ffn_maa_k, ffn_maa_r, Wfk, Wfr, Wfv):
        import jax, jax.numpy as jnp
        import numpy as np
        E, H, L, B = (512, 32, 256, 4)
        S = E // H
        DM, DD = (32, 64)

        def _ln(x, w, b, eps=1e-05):
            m = x.mean(-1, keepdims=True)
            v = ((x - m) ** 2).mean(-1, keepdims=True)
            return (x - m) / jnp.sqrt(v + eps) * w + b

        def _block(x, state, ln1_w, ln1_b, ln2_w, ln2_b, maa_x, maa_w1, maa_w2, maa_stack, time_decay, td_w1, td_w2, u, Wr, Wk, Wv, Wg, Wo, gn_w, gn_b, ffn_maa_k, ffn_maa_r, Wfk, Wfr, Wfv):
            b, l, e = x.shape
            h = u.shape[0]
            s_ = e // h
            xa = _ln(x, ln1_w, ln1_b)
            sx = jnp.concatenate([state[:, 1:2] - xa[:, :1], xa[:, :-1] - xa[:, 1:]], axis=1)
            xxx = jnp.tanh((xa + sx * maa_x) @ maa_w1).reshape(b, l, 5, DM)
            xxx = jnp.einsum('blfd,fde->blfe', xxx, maa_w2)
            xm = xa[:, :, None] + sx[:, :, None] * (maa_stack + xxx)
            xk, xw, xv, xr, xg = (xm[:, :, j] for j in range(5))
            w = jnp.exp(-jnp.exp(time_decay + jnp.tanh(xw @ td_w1) @ td_w2)).reshape(b, l, h, s_)
            r = (xr @ Wr.T).reshape(b, l, h, s_)
            k = (xk @ Wk.T).reshape(b, l, h, s_)
            v = (xv @ Wv.T).reshape(b, l, h, s_)
            g = jax.nn.silu(xg @ Wg.T)
            s0 = state[:, 2:2 + s_].reshape(b, h, s_, s_)

            def step(s, rkvw):
                r_t, k_t, v_t, w_t = rkvw
                a = k_t[..., :, None] * v_t[..., None, :]
                out = jnp.einsum('bhi,bhij->bhj', r_t, u * a + s)
                s = a + w_t[..., :, None] * s
                return (s, out)
            rkvw = tuple((jnp.moveaxis(t, 1, 0) for t in (r, k, v, w)))
            _, out = jax.lax.scan(step, s0, rkvw)
            out = jnp.moveaxis(out, 0, 1).reshape(b, l, e)
            og = out.reshape(b, l, h, s_)
            m = og.mean(-1, keepdims=True)
            va = ((og - m) ** 2).mean(-1, keepdims=True)
            og = ((og - m) / jnp.sqrt(va + 1e-05)).reshape(b, l, e) * gn_w + gn_b
            x1 = x + og * g @ Wo.T
            xc = _ln(x1, ln2_w, ln2_b)
            sx2 = jnp.concatenate([state[:, 0:1] - xc[:, :1], xc[:, :-1] - xc[:, 1:]], axis=1)
            xk2 = xc + sx2 * ffn_maa_k
            xr2 = xc + sx2 * ffn_maa_r
            rr = jax.nn.sigmoid(xr2 @ Wfr.T)
            kk = jnp.square(jax.nn.relu(xk2 @ Wfk.T))
            return x1 + rr * (kk @ Wfv.T)
        return _block(x, state, ln1_w, ln1_b, ln2_w, ln2_b, maa_x, maa_w1, maa_w2, maa_stack, time_decay, td_w1, td_w2, u, Wr, Wk, Wv, Wg, Wo, gn_w, gn_b, ffn_maa_k, ffn_maa_r, Wfk, Wfr, Wfv)
    x = _L0_xattn_ref(x, ctx_2048, L0_xattn_Wq, L0_xattn_bq, L0_xattn_Wk, L0_xattn_bk, L0_xattn_Wv, L0_xattn_bv)
    x = _L1_xattn_ref(x, ctx_2048, L1_xattn_ln1_w, L1_xattn_ln1_b, L1_xattn_ln2_w, L1_xattn_ln2_b, L1_xattn_maa_x, L1_xattn_maa_w1, L1_xattn_maa_w2, L1_xattn_maa_stack, L1_xattn_time_decay, L1_xattn_td_w1, L1_xattn_td_w2, L1_xattn_u, L1_xattn_Wr, L1_xattn_Wk, L1_xattn_Wv, L1_xattn_Wg, L1_xattn_Wo, L1_xattn_gn_w, L1_xattn_gn_b, L1_xattn_ffn_maa_k, L1_xattn_ffn_maa_r, L1_xattn_Wfk, L1_xattn_Wfr, L1_xattn_Wfv)
    return x

_drawn_inputs = setup_inputs


def setup_inputs(seed=0):
    import zlib

    import numpy as np

    out = dict(_drawn_inputs(seed))
    spreads = {'L1_xattn_ln1_w': (1.0, 0.2),
     'L1_xattn_ln1_b': (0.0, 0.292),
     'L1_xattn_ln2_w': (1.0, 0.6),
     'L1_xattn_ln2_b': (0.0, 0.8),
     'L1_xattn_gn_w': (1.0, 0.6),
     'L1_xattn_gn_b': (0.0, 0.742)}
    factors = {'L0_xattn_bk': 8.0,
     'L1_xattn_maa_x': 8.0,
     'L1_xattn_maa_w1': 3.13,
     'L1_xattn_maa_w2': 3.077,
     'L1_xattn_td_w1': 8.0,
     'L1_xattn_td_w2': 8.0,
     'L1_xattn_u': 3.189,
     'L1_xattn_ffn_maa_k': 6.046,
     'L1_xattn_ffn_maa_r': 8.0,
     'L1_xattn_Wfr': 4.354}
    for name, (base, spread) in spreads.items():
        noise = np.random.default_rng([zlib.crc32(name.encode()), seed]).standard_normal(out[name].shape)
        drawn = base * np.exp(spread * noise) if base else spread * noise
        out[name] = jnp.asarray(drawn.astype(out[name].dtype))
    for name, factor in factors.items():
        out[name] = (out[name] * factor).astype(out[name].dtype)
    return out
```

```python
from contextlib import ExitStack

import concourse.bass as bass
from concourse import mybir

ALU = mybir.AluOpType
ACT = mybir.ActivationFunctionType
AX_X = mybir.AxisListType.X
F32 = mybir.dt.float32

P = 128
B, TOK, E = 8, 256, 512
CT = TOK // P
NT = E // P
DQ = 32
H, D = 32, 16
SL = E // P
G = D // SL
DM, DD = 32, 64
NMIX = 5
MIX_K, MIX_W, MIX_V, MIX_R, MIX_G = range(NMIX)
MIX_ORDER = [MIX_W, MIX_K, MIX_V, MIX_R, MIX_G]
ROW = TOK + 1
NCH = G * SL
NS = 6
EPS = 1e-5

FRONT_USES = ["qk", "v0", "s01", "s23", "t01", "t23", "out", "xnT", "w1",
              "m1", "m0", "td1", "k", "td2", "m2", "v", "m3", "r", "rep0", "rep1", "rep2", "rep3", "m4", "g"]
NF = len(FRONT_USES)
USE = {n: i for i, n in enumerate(FRONT_USES)}
BACK0_USES = ["bonus", "mean", "wo", "fk", "fv"]
BACK1_USES = ["y", "var", "xcT", "fr"]

_INS = ["x", "ctx", "wq", "wk", "wv", "bq", "bk", "bv", "ident", "rep", "red", "head_sum", "head_mean",
        "ln1_w", "ln1_b", "maa_x", "maa_stack", "maa_w1", "maa_w2", "td_w1", "td_w2", "time_decay", "u",
        "Wr", "Wk", "Wv", "Wg", "Wo", "gn_w", "gn_b", "ln2_w", "ln2_b", "ffn_k", "ffn_r", "Wfk", "Wfr", "Wfv"]


def xattn_rwkv_kernel(nc, io, out_dram):
    with ExitStack() as ctx:
        def sb(name, *shape):
            return ctx.enter_context(nc.sbuf_tensor(name, list(shape), F32))

        def psum(name, *shape):
            return ctx.enter_context(nc.psum_tensor(name, list(shape), F32))

        def sem(name):
            return ctx.enter_context(nc.semaphore(name))

        wq, wk = sb("wq", P, CT, DQ), sb("wk", P, CT, DQ)
        wv = sb("wv", P, CT, TOK)
        bq, bk, bv = sb("bq", DQ, 1), sb("bk", DQ, 1), sb("bv", P, CT)
        ident = sb("ident", P, P)
        rep = sb("rep", P, G, P)
        red = sb("red", P, H)
        head_sum, head_mean = sb("head_sum", P, P), sb("head_mean", P, P)
        vecs = {n: sb(n, P, SL) for n in ["ln1_w", "ln1_b", "maa_x", "time_decay", "u", "gn_w", "gn_b",
                                          "ln2_w", "ln2_b", "ffn_k", "ffn_r"]}
        maa_stack = sb("maa_stack", P, NMIX, SL)
        maa_w1 = sb("maa_w1", P, SL, NMIX * DM)
        maa_w2a = sb("maa_w2a", P, SL, P)
        low_rank = sb("low_rank", DD + DM, SL, P)
        td_w2, maa_w2b = low_rank[0:DD], low_rank[DD:DD + DM]
        td_w1 = sb("td_w1", P, SL, DD)
        w_proj = {n: sb(n, P, SL, SL, P) for n in ["Wr", "Wk", "Wv", "Wg", "Wfk"]}
        w_tok = {n: sb(n, P, SL, E) for n in ["Wo", "Wfr", "Wfv"]}
        wait_col = sb("wait_col", P, 1)
        eps_col = sb("eps_col", P, 1)
        half_neg = sb("half_neg", P, 1)

        x_in, ctx_in = sb("x_in", P, CT, E), sb("ctx_in", P, CT, E)
        prev_att, prev_ffn = sb("prev_att", P, SL), sb("prev_ffn", P, SL)
        state0 = sb("state0", P, SL * D)
        reg_a = sb("reg_a", P, NT, E)
        reg_b = sb("reg_b", P, NT, E)
        reg_c = sb("reg_c", P, NT, TOK)
        reg_d = sb("reg_d", P, 2, E)
        x_mid, x_res = sb("x_mid", P, CT, E), sb("x_res", P, CT, E)
        xa, xc = sb("xa", P, SL, ROW), sb("xc", P, SL, ROW)
        sx = sb("sx", P, SL, TOK)
        h_a = sb("h_a", P, TOK)
        low_act = sb("low_act", DD + DM, TOK)
        tw, h_b = low_act[0:DD], low_act[DD:DD + DM]
        decay = sb("decay", P, SL, 2, ROW)
        vrep = sb("vrep", P, G, SL, TOK)
        k_sb, v_sb, r_sb, gate = (sb(n, P, SL, TOK) for n in ["k_sb", "v_sb", "r_sb", "gate"])
        states = sb("states", P, NS, SL, ROW)
        y = sb("y", P, SL, TOK)
        rstd = sb("rstd", P, TOK)
        score_max, row_sum, row_inv = sb("score_max", P, NT), sb("row_sum", P, NT), sb("row_inv", P, NT)
        ln_stat, ln_mv, ln_var, ln_rstd = sb("ln_stat", P, CT, 6), sb("ln_mv", P, CT, 2), sb("ln_var", P, CT), sb("ln_rstd", P, CT)

        attn, attnT = reg_a, reg_b
        xn = reg_a[:, 0:2, :]
        xpre = reg_a[:, 2:4, :].rearrange("p a (c t) -> p (a c) t", t=TOK)
        xk2 = reg_a[:, 0:2, :].rearrange("p a (c t) -> p (a c) t", t=TOK)
        xr2 = xpre
        kk = reg_b[:, 0:2, :].rearrange("p a (c t) -> p (a c) t", t=TOK)
        o_sb = reg_b[:, 2:4, :]
        vT = reg_c
        xn2 = reg_c[:, :, :].rearrange("p (c a) t -> p c (a t)", c=CT)
        sx2 = reg_c
        qk = reg_d[0:DQ, :, :]
        sq = reg_d[:, :, :].rearrange("p a (c t) -> p (a c) t", t=TOK)
        bonus_v = sq
        bonus = y
        rate = states[:, 0, :, 0:TOK]
        xm = [states[:, 1, :, 0:TOK], states[:, 2, :, 0:TOK]]

        front = [psum("front0", P, 1024), psum("front1", P, 1024)]
        back = [psum("back0", P, 1024), psum("back1", P, 1024)]

        def slots(ps):
            return ps[:, :].rearrange("p (s t) -> p s t", t=TOK)

        def halves(ps):
            return ps[:, :].rearrange("p (c n) -> p c n", c=2)

        w_l0, w_mix, w_wkv, w_back = sem("w_l0"), sem("w_mix"), sem("w_wkv"), sem("w_back")
        x_landed, ctx_landed, prev_att_landed = sem("x_landed"), sem("ctx_landed"), sem("prev_att_landed")
        prev_ffn_landed, state_landed, out_stored = sem("prev_ffn_landed"), sem("state_landed"), sem("out_stored")
        consts_set = sem("consts_set")
        front_filled = sem("front_filled")
        back_filled = {u: sem(f"{u}_filled") for u in BACK0_USES + BACK1_USES if u != "y"}
        qk_ready = sem("qk_ready")
        vT_ready = sem("vT_ready")
        max_ready = sem("max_ready")
        exp_ready = sem("exp_ready")
        inv_ready = sem("inv_ready")
        attn_ready = sem("attn_ready")
        attnT_act, attnT_vec = sem("attnT_act"), sem("attnT_vec")
        x_mid_ready = sem("x_mid_ready")
        stat_ready = sem("stat_ready")
        mv_ready = sem("mv_ready")
        lvar_ready = sem("lvar_ready")
        lrstd_ready = sem("lrstd_ready")
        xn_ready = sem("xn_ready")
        xa_ready = sem("xa_ready")
        sx_ready = sem("sx_ready")
        xpre_ready = sem("xpre_ready")
        h_ready = sem("h_ready")
        mixed = sem("mixed")
        xm_ready = sem("xm_ready")
        tw_ready = sem("tw_ready")
        rate_ready = sem("rate_ready")
        decay_ready = sem("decay_ready")
        k_ready, v_ready, r_ready = sem("k_ready"), sem("v_ready"), sem("r_ready")
        vrep_ready = sem("vrep_ready")
        th_ready, gate_ready = sem("th_ready"), sem("gate_ready")
        res_ready = sem("res_ready")
        bonus_ready = sem("bonus_ready")
        kv_ready, row0_ready, scanned = sem("kv_ready"), sem("row0_ready"), sem("scanned")
        prod_ready, reduced = sem("prod_ready"), sem("reduced")
        bonus_v_ready, y_ready = sem("bonus_v_ready"), sem("y_ready")
        centred, sq_ready, gvar_ready, grstd_ready = sem("centred"), sem("sq_ready"), sem("gvar_ready"), sem("grstd_ready")
        normed, affine, gated = sem("normed"), sem("affine"), sem("gated")
        x1_ready = sem("x1_ready")
        stat2_ready, mv2_ready, lvar2_ready, lrstd2_ready = sem("stat2_ready"), sem("mv2_ready"), sem("lvar2_ready"), sem("lrstd2_ready")
        xn2_ready = sem("xn2_ready")
        xc_ready = sem("xc_ready")
        sx2_ready, xk2_ready, xr2_ready = sem("sx2_ready"), sem("xk2_ready"), sem("xr2_ready")
        relu_ready, kk_ready = sem("relu_ready"), sem("kk_ready")
        rr_ready, gated_ffn, out_ready = sem("rr_ready"), sem("gated_ffn"), sem("out_ready")

        block = ctx.enter_context(nc.Block())

        def later(b):
            return not (isinstance(b, int) and b == 0)

        def filled(b, use):
            return b * NF + USE[use] + 1

        def front_unit(use):
            return front[USE[use] % 2]

        FRONT_DRAINED = {
            "qk": (qk_ready, 2, 2), "v0": (vT_ready, 1, 1), "s01": (exp_ready, NT, 2), "s23": (exp_ready, NT, NT),
            "t01": (attnT_act, 1, 1), "t23": (attnT_vec, 1, 1), "out": (x_mid_ready, CT, CT), "xnT": (xa_ready, 1 + SL, 1 + SL),
            "w1": (h_ready, 2, 2), "td1": (tw_ready, 1, 1), "td2": (rate_ready, SL, SL),
            "k": (k_ready, 1, 1), "v": (v_ready, 1, 1), "r": (r_ready, 1, 1), "g": (gate_ready, 1, 1)}
        FRONT_DRAINED.update({f"m{f}": (mixed, NMIX, n + 1) for n, f in enumerate(MIX_ORDER)})
        FRONT_DRAINED.update({f"rep{g}": (vrep_ready, G, g + 1) for g in range(G)})
        BACK_DRAINED = {
            "bonus": (bonus_v_ready, 1, 1), "mean": (centred, 1, 1), "wo": (x1_ready, 1, 1), "fk": (relu_ready, 1, 1),
            "fv": (gated_ffn, 1, 1), "y": (y_ready, 1, 1), "var": (gvar_ready, 1, 1), "xcT": (xc_ready, 1 + SL, 1 + SL),
            "fr": (rr_ready, 1, 1)}

        def has_former(b, use):
            return later(b) or USE[use] >= 2

        def former_drained(b, use):
            before = USE[use] - 2
            s, per, n = FRONT_DRAINED[FRONT_USES[before % NF]]
            return (s, b * per + n) if before >= 0 else (s, b * per)

        def back_uses(use):
            return (0, BACK0_USES) if use in BACK0_USES else (1, BACK1_USES)

        def back_unit(use):
            return back[back_uses(use)[0]]

        def has_former_back(b, use):
            return later(b) or back_uses(use)[1].index(use) > 0

        def former_drained_back(b, use):
            names = back_uses(use)[1]
            before = names.index(use) - 1
            s, per, n = BACK_DRAINED[names[before]]
            return (s, b * per + n) if before >= 0 else (s, b * per)

        @block.sync
        def _(sp):
            def load(dst, name, s):
                sp.dma_start(dst, io[name]).then_inc(s, 16)

            def by_group(row, n):
                return row.rearrange("(h g n) -> g h n", g=G, n=n)

            def load_sequence(b):
                if later(b):
                    sp.wait_ge(x_mid_ready, b * CT)
                sp.dma_start(x_in[:, :, :], io["x"][b, :, :].rearrange("(c p) n -> p c n", p=P)).then_inc(x_landed, 16)
                sp.dma_start(ctx_in[:, :, :], io["ctx"][b, :, :].rearrange("(c p) n -> p c n", p=P)).then_inc(ctx_landed, 16)
                if later(b):
                    sp.wait_ge(xa_ready, b * (1 + SL))
                for g in range(G):
                    sp.dma_start(prev_att[H * g:H * (g + 1), :], by_group(io["ctx"][b, 1, :], SL)[g]).then_inc(prev_att_landed, 16)
                if later(b):
                    sp.wait_ge(row0_ready, b * NCH)
                for g in range(G):
                    sp.dma_start(state0[H * g:H * (g + 1), :], by_group(io["ctx"][b, 2:2 + D, :].rearrange("r e -> (r e)"), SL * D)[g])\
                        .then_inc(state_landed, 16)
                if later(b):
                    sp.wait_ge(xc_ready, b * (1 + SL))
                for g in range(G):
                    sp.dma_start(prev_ffn[H * g:H * (g + 1), :], by_group(io["ctx"][b, 0, :], SL)[g]).then_inc(prev_ffn_landed, 16)

            for name, dst in [("wq", wq), ("wk", wk), ("bq", bq), ("bk", bk)]:
                load(dst[:], name, w_l0)
            load_sequence(0)
            for name, dst in [("wv", wv), ("bv", bv), ("ident", ident)]:
                load(dst[:], name, w_l0)
            for name in ["ln1_w", "ln1_b", "maa_x", "time_decay", "u"]:
                load(vecs[name][:], name, w_mix)
            load(maa_stack[:], "maa_stack", w_mix)
            load(maa_w1[:], "maa_w1", w_mix)
            sp.dma_start(maa_w2a[:], io["maa_w2"][0:P, :, :]).then_inc(w_mix, 16)
            sp.dma_start(maa_w2b[:], io["maa_w2"][P:P + DM, :, :]).then_inc(w_mix, 16)
            load(td_w1[:], "td_w1", w_mix)
            load(td_w2[:], "td_w2", w_mix)
            for name in ["Wk", "Wv", "Wr", "Wg"]:
                load(w_proj[name][:], name, w_wkv)
            for name, dst in [("rep", rep), ("red", red), ("head_sum", head_sum)]:
                load(dst[:], name, w_wkv)
            load(head_mean[:], "head_mean", w_back)
            for name in ["gn_w", "gn_b", "ln2_w", "ln2_b", "ffn_k", "ffn_r"]:
                load(vecs[name][:], name, w_back)
            for name in ["Wo", "Wfr", "Wfv"]:
                load(w_tok[name][:], name, w_back)
            load(w_proj["Wfk"][:], "Wfk", w_back)
            with sp.Fori(1, B) as b:
                load_sequence(b)
            sp.wait_ge(out_stored, 16 * B)

        W_L0, W_MIX, W_WKV, W_BACK = 16 * 7, 16 * 11, 16 * 7, 16 * 11

        @block.tensor
        def _(pe):
            mm = nc.tensor.matmul

            def front_qkv(b):
                pe.wait_ge(x_landed, (b + 1) * 16)
                pe.wait_ge(ctx_landed, (b + 1) * 16)
                if has_former(b, "qk"):
                    pe.wait_ge(*former_drained(b, "qk"))
                ps = front_unit("qk")
                for half, w, src in ((0, wq, x_in), (1, wk, ctx_in)):
                    for c in range(CT):
                        last = mm(ps[0:DQ, half * E:(half + 1) * E], w[:, c, :], src[:, c, :], start=(c == 0), stop=(c == CT - 1))
                last.then_inc(front_filled, 1)
                if has_former(b, "v0"):
                    pe.wait_ge(*former_drained(b, "v0"))
                ps = slots(front_unit("v0"))
                for m in range(NT):
                    for c in range(CT):
                        last = mm(ps[:, m, :], ctx_in[:, c, m * P:(m + 1) * P], wv[:, c, :], start=(c == 0), stop=(c == CT - 1))
                last.then_inc(front_filled, 1)

            def front_scores(b):
                pe.wait_ge(qk_ready, (b + 1) * 2)
                for use, n0 in (("s01", 0), ("s23", 2)):
                    if has_former(b, use):
                        pe.wait_ge(*former_drained(b, use))
                    ps = halves(front_unit(use))
                    for n in (n0, n0 + 1):
                        last = mm(ps[:, n - n0, :], qk[:, 0, n * P:(n + 1) * P], qk[:, 1, :], start=True, stop=True)
                    last.then_inc(front_filled, 1)

            def front_transposes(b):
                pe.wait_ge(attn_ready, (b + 1) * NT)
                for use, m0 in (("t01", 0), ("t23", 2)):
                    if has_former(b, use):
                        pe.wait_ge(*former_drained(b, use))
                    ps = halves(front_unit(use))
                    for m in (m0, m0 + 1):
                        for n in range(NT):
                            last = nc.tensor.transpose(ps[:, m - m0, n * P:(n + 1) * P], attn[:, n, m * P:(m + 1) * P], ident[:, :])
                    last.then_inc(front_filled, 1)

            def front_out(b):
                pe.wait_ge(vT_ready, b + 1)
                pe.wait_ge(attnT_act, b + 1)
                pe.wait_ge(attnT_vec, b + 1)
                if has_former(b, "out"):
                    pe.wait_ge(*former_drained(b, "out"))
                ps = halves(front_unit("out"))
                for c in range(CT):
                    for m in range(NT):
                        last = mm(ps[:, c, :], vT[:, m, c * P:(c + 1) * P], attnT[:, m, :], start=(m == 0), stop=(m == NT - 1))
                last.then_inc(front_filled, 1)

            def front_xnT(b):
                pe.wait_ge(xn_ready, (b + 1) * CT)
                if has_former(b, "xnT"):
                    pe.wait_ge(*former_drained(b, "xnT"))
                ps = slots(front_unit("xnT"))
                for s in range(SL):
                    for c in range(CT):
                        last = nc.tensor.transpose(ps[:, s, c * P:(c + 1) * P], xn[:, c, s * P:(s + 1) * P], ident[:, :])
                last.then_inc(front_filled, 1)

            def front_w1(b):
                pe.wait_ge(xpre_ready, (b + 1) * SL)
                if has_former(b, "w1"):
                    pe.wait_ge(*former_drained(b, "w1"))
                ps = front_unit("w1")
                for lo, hi, p0, off in ((0, P, 0, 0), (P, NMIX * DM, DD, E)):
                    for s in range(SL):
                        last = mm(ps[p0:p0 + hi - lo, off:off + TOK], maa_w1[:, s, lo:hi], xpre[:, s, :], start=(s == 0), stop=(s == SL - 1))
                last.then_inc(front_filled, 1)

            def mix(b, f):
                if f == MIX_ORDER[0]:
                    pe.wait_ge(h_ready, (b + 1) * 2)
                if has_former(b, f"m{f}"):
                    pe.wait_ge(*former_drained(b, f"m{f}"))
                ps = slots(front_unit(f"m{f}"))
                lo = f * DM % P
                w2, h = (maa_w2a, h_a) if f * DM < P else (maa_w2b, h_b)
                for s in range(SL):
                    last = mm(ps[:, s, :], w2[lo:lo + DM, s, :], h[lo:lo + DM, :], start=True, stop=True)
                last.then_inc(front_filled, 1)

            def project(b, use, w, f):
                n = MIX_ORDER.index(f)
                pe.wait_ge(xm_ready, b * NMIX + n + 1)
                if has_former(b, use):
                    pe.wait_ge(*former_drained(b, use))
                ps = slots(front_unit(use))
                for o in range(SL):
                    for s in range(SL):
                        last = mm(ps[:, o, :], w[:, s, o, :], xm[n % 2][:, s, :], start=(s == 0), stop=(s == SL - 1))
                last.then_inc(front_filled, 1)

            def td_hidden(b):
                pe.wait_ge(xm_ready, b * NMIX + 1)
                if has_former(b, "td1"):
                    pe.wait_ge(*former_drained(b, "td1"))
                ps = front_unit("td1")
                for s in range(SL):
                    last = mm(ps[0:DD, 0:TOK], td_w1[:, s, :], xm[0][:, s, :], start=(s == 0), stop=(s == SL - 1))
                last.then_inc(front_filled, 1)

            def td_out(b):
                pe.wait_ge(tw_ready, b + 1)
                if has_former(b, "td2"):
                    pe.wait_ge(*former_drained(b, "td2"))
                ps = slots(front_unit("td2"))
                for s in range(SL):
                    last = mm(ps[:, s, :], td_w2[:, s, :], tw[:, :], start=True, stop=True)
                last.then_inc(front_filled, 1)

            def replicate(b, g):
                pe.wait_ge(v_ready, b + 1)
                if has_former(b, f"rep{g}"):
                    pe.wait_ge(*former_drained(b, f"rep{g}"))
                ps = halves(front_unit(f"rep{g}"))
                for c in range(2):
                    last = mm(ps[:, c, :], rep[:, g, :], v_sb[:, 2 * c:2 * c + 2, :].rearrange("p a t -> p (a t)"), start=True, stop=True)
                last.then_inc(front_filled, 1)

            def wkv_bonus(b):
                pe.wait_ge(bonus_ready, (b + 1) * SL)
                if has_former_back(b, "bonus"):
                    pe.wait_ge(*former_drained_back(b, "bonus"))
                ps = back_unit("bonus")
                for s in range(SL):
                    last = mm(ps[:, 0:TOK], head_sum[:, :], bonus[:, s, :], start=(s == 0), stop=(s == SL - 1))
                last.then_inc(back_filled["bonus"], 1)

            def wkv_reduce(b, s):
                pe.wait_ge(prod_ready, b * NCH + G * (s + 1))
                if s == 0 and has_former_back(b, "y"):
                    pe.wait_ge(*former_drained_back(b, "y"))
                ps = back_unit("y")
                for half in range(2):
                    for g in range(G):
                        chunk = states[:, (s * G + g) % NS, 2 * half:2 * half + 2, 0:TOK]
                        last = mm(ps[H * g:H * (g + 1), half * 2 * TOK:(half + 1) * 2 * TOK], red[:, :], chunk,
                                  start=(s == 0), stop=(s == SL - 1))
                last.then_inc(reduced, 1)

            def head_mean_of(b, use, src):
                if has_former_back(b, use):
                    pe.wait_ge(*former_drained_back(b, use))
                ps = back_unit(use)
                for s in range(SL):
                    last = mm(ps[:, 0:TOK], head_mean[:, :], src[:, s, :], start=(s == 0), stop=(s == SL - 1))
                last.then_inc(back_filled[use], 1)

            def tok_product(b, use, x, w):
                if has_former_back(b, use):
                    pe.wait_ge(*former_drained_back(b, use))
                ps = halves(back_unit(use))
                for c in range(CT):
                    for s in range(SL):
                        last = mm(ps[:, c, :], x[:, s, c * P:(c + 1) * P], w[:, s, :], start=(s == 0), stop=(s == SL - 1))
                last.then_inc(back_filled[use], 1)

            def back_mean(b):
                pe.wait_ge(y_ready, b + 1)
                head_mean_of(b, "mean", y)

            def back_var(b):
                pe.wait_ge(sq_ready, b + 1)
                head_mean_of(b, "var", sq)

            def back_wo(b):
                pe.wait_ge(gated, b + 1)
                tok_product(b, "wo", y, w_tok["Wo"])

            def back_xcT(b):
                pe.wait_ge(xn2_ready, (b + 1) * CT)
                if has_former_back(b, "xcT"):
                    pe.wait_ge(*former_drained_back(b, "xcT"))
                ps = slots(back_unit("xcT"))
                for s in range(SL):
                    for c in range(CT):
                        last = nc.tensor.transpose(ps[:, s, c * P:(c + 1) * P], xn2[:, c, s * P:(s + 1) * P], ident[:, :])
                last.then_inc(back_filled["xcT"], 1)

            def back_fk(b):
                pe.wait_ge(xk2_ready, (b + 1) * SL)
                if has_former_back(b, "fk"):
                    pe.wait_ge(*former_drained_back(b, "fk"))
                ps = slots(back_unit("fk"))
                for o in range(SL):
                    for s in range(SL):
                        last = mm(ps[:, o, :], w_proj["Wfk"][:, s, o, :], xk2[:, s, :], start=(s == 0), stop=(s == SL - 1))
                last.then_inc(back_filled["fk"], 1)

            def back_fr(b):
                pe.wait_ge(xr2_ready, (b + 1) * SL)
                tok_product(b, "fr", xr2, w_tok["Wfr"])

            def back_fv(b):
                pe.wait_ge(kk_ready, b + 1)
                tok_product(b, "fv", kk, w_tok["Wfv"])

            def front1_step(b, c):
                if c == 0: front_qkv(b)
                if c == 2: front_scores(b)
                if c == 7: front_transposes(b)
                if c == 9: front_out(b)
                if c == 12: front_xnT(b)
                if c == 15: front_w1(b)

            def phase2(b, nb):
                front, back_ = nb is not None, b is not None
                if back_: back_mean(b)
                if front: mix(nb, MIX_W); mix(nb, MIX_K)
                if back_: back_var(b)
                if front: td_hidden(nb); project(nb, "k", w_proj["Wk"], MIX_K)
                if front: td_out(nb)
                if front: mix(nb, MIX_V)
                if back_: back_wo(b)
                if front: project(nb, "v", w_proj["Wv"], MIX_V)
                if front: mix(nb, MIX_R)
                if back_: back_xcT(b)
                if front: project(nb, "r", w_proj["Wr"], MIX_R)
                if front: [replicate(nb, g) for g in range(G)]
                if back_: back_fk(b); back_fr(b)
                if front: mix(nb, MIX_G)
                if back_: back_fv(b)
                if front: project(nb, "g", w_proj["Wg"], MIX_G)

            def phase1(b, nb):
                wkv_bonus(b)
                for c in range(NCH):
                    if c % G == G - 1:
                        wkv_reduce(b, c // G)
                    if nb is not None:
                        front1_step(nb, c)

            pe.wait_ge(w_l0, W_L0)
            for c in range(NCH):
                if c == 12: pe.wait_ge(w_mix, W_MIX)
                front1_step(0, c)
            pe.wait_ge(w_wkv, W_WKV)
            phase2(None, 0)
            pe.wait_ge(w_back, W_BACK)
            phase1(0, 1)
            phase2(0, 1)
            with pe.Fori(1, B - 1) as b:
                phase1(b, b + 1)
                phase2(b, b + 1)
            phase1(B - 1, None)
            phase2(B - 1, None)

        @block.vector
        def _(dve):
            v = nc.vector

            def front_scores(b):
                for use, n0 in (("s01", 0), ("s23", 2)):
                    dve.wait_ge(front_filled, filled(b, use))
                    ps = halves(front_unit(use))
                    for n in (n0, n0 + 1):
                        if later(b):
                            dve.wait_ge(attn_ready, b * NT)
                        v.tensor_reduce(score_max[:, n:n + 1], ps[:, n - n0, :], AX_X, ALU.max, negate=True).then_inc(max_ready, 1)

            def front_normalise(b):
                for n in range(NT):
                    dve.wait_ge(exp_ready, b * NT + n + 1)
                    v.reciprocal(row_inv[:, n:n + 1], row_sum[:, n:n + 1]).then_inc(inv_ready, 1)
                    dve.wait_ge(inv_ready, b * NT + n + 1)
                    v.tensor_scalar(attn[:, n, :], attn[:, n, :], row_inv[:, n:n + 1], None, ALU.mult).then_inc(attn_ready, 1)

            def front_attnT(b, stored):
                if stored is not None:
                    dve.wait_ge(out_stored, stored * 16)
                dve.wait_ge(front_filled, filled(b, "t23"))
                ps = halves(front_unit("t23"))
                v.tensor_copy(attnT[:, 2:4, :], ps).then_inc(attnT_vec, 1)

            def layer_norm(b, x, dst, stat_s, mv_s, lvar_s, lrstd_s, out_s):
                for c in range(CT):
                    v.bn_stats(ln_stat[:, c, :], x[:, c, :]).then_inc(stat_s, 1)
                dve.wait_ge(stat_s, (b + 1) * CT)
                v.memset(wait_col[:, :], 0.0)
                for c in range(CT):
                    v.bn_aggr(ln_mv[:, c, :], ln_stat[:, c, :]).then_inc(mv_s, 1)
                dve.wait_ge(mv_s, (b + 1) * CT)
                v.tensor_scalar(ln_var[:, :], ln_mv[:, :, 1], EPS, None, ALU.add).then_inc(lvar_s, 1)
                dve.wait_ge(lrstd_s, b + 1)
                for c in range(CT):
                    v.tensor_scalar(dst[:, c, :].rearrange("p (s g h) -> p h g s", s=SL, g=G),
                                    x[:, c, :].rearrange("p (h g s) -> p h g s", s=SL, g=G), ln_mv[:, c, 0:1], ln_rstd[:, c:c + 1], ALU.subtract, ALU.mult).then_inc(out_s, 1)

            def front_ln(b):
                dve.wait_ge(front_filled, filled(b, "out"))
                ps = halves(front_unit("out"))
                if later(b):
                    dve.wait_ge(res_ready, b)
                for c in range(CT):
                    ins = v.scalar_tensor_tensor(x_mid[:, c, :], ps[:, c, :], bv[:, c:c + 1], x_in[:, c, :], ALU.add, ALU.add)
                    ins.then_inc(x_mid_ready, 1)
                dve.wait_ge(x_mid_ready, (b + 1) * CT)
                layer_norm(b, x_mid, xn, stat_ready, mv_ready, lvar_ready, lrstd_ready, xn_ready)

            def front_shift(b):
                dve.wait_ge(xa_ready, (b + 1) * (1 + SL))
                v.tensor_tensor(sx[:, :, :], xa[:, :, 0:TOK], xa[:, :, 1:ROW], ALU.subtract).then_inc(sx_ready, 1)
                dve.wait_ge(sx_ready, b + 1)
                for s in range(SL):
                    v.scalar_tensor_tensor(xpre[:, s, :], sx[:, s, :], vecs["maa_x"][:, s:s + 1], xa[:, s, 1:ROW], ALU.mult, ALU.add)\
                        .then_inc(xpre_ready, 1)

            def mix(b, f):
                n = MIX_ORDER.index(f)
                dve.wait_ge(front_filled, filled(b, f"m{f}"))
                ps = slots(front_unit(f"m{f}"))
                if n >= 2:
                    dve.wait_ge(front_filled, b * NF + USE[{MIX_W: "td1", MIX_K: "k", MIX_V: "v"}[MIX_ORDER[n - 2]]] + 1)
                elif not (isinstance(b, int) and b == 0):
                    if later(b):
                        dve.wait_ge(reduced, b * SL)
                for s in range(SL):
                    last = v.scalar_tensor_tensor(xm[n % 2][:, s, :], ps[:, s, :], maa_stack[:, f, s:s + 1], sx[:, s, :], ALU.add, ALU.mult)
                last.then_inc(mixed, 1)

            def front_gate(b):
                dve.wait_ge(front_filled, filled(b, "g"))
                ps = front_unit("g")
                dve.wait_ge(th_ready, b + 1)
                g2 = gate[:, :, :].rearrange("p s t -> p (s t)")
                v.scalar_tensor_tensor(g2, g2, 1.0, ps[:, :], ALU.add, ALU.mult).then_inc(gate_ready, 1)

            def wkv_bonus(b):
                dve.wait_ge(k_ready, b + 1)
                dve.wait_ge(r_ready, b + 1)
                if later(b):
                    dve.wait_ge(gated_ffn, b)
                for s in range(SL):
                    v.scalar_tensor_tensor(bonus[:, s, :], r_sb[:, s, :], vecs["u"][:, s:s + 1], k_sb[:, s, :], ALU.mult, ALU.mult)\
                        .then_inc(bonus_ready, 1)

            def wkv_kv(b, c):
                s, g = divmod(c, G)
                if s == 0:
                    dve.wait_ge(vrep_ready, b * G + g + 1)
                if c >= NS:
                    dve.wait_ge(reduced, b * SL + (c - NS) // G + 1)
                elif c == 0:
                    dve.wait_ge(decay_ready, (b + 1) * SL)
                    dve.wait_ge(front_filled, filled(b, "g"))
                k_row = k_sb[:, s, :].unsqueeze(1).to_broadcast([P, SL, TOK])
                v.tensor_tensor(states[:, c % NS, :, 1:ROW], vrep[:, g, :, :], k_row, ALU.mult).then_inc(kv_ready, 1)

            def wkv_scan(b, c):
                s = c // G
                dve.wait_ge(kv_ready, b * NCH + c + 1)
                dve.wait_ge(row0_ready, b * NCH + c + 1)
                w2 = decay[:, s, :, :].rearrange("p a t -> p (a t)")
                for half in range(2):
                    st = states[:, c % NS, 2 * half:2 * half + 2, :].rearrange("p a t -> p (a t)")
                    v.tensor_tensor_scan(st, w2, st, 0.0, ALU.mult, ALU.add).then_inc(scanned, 1)

            def wkv_prod(b, c):
                dve.wait_ge(scanned, b * 2 * NCH + 2 * c + 2)
                r_row = r_sb[:, c // G, :].unsqueeze(1).to_broadcast([P, SL, TOK])
                st = states[:, c % NS, :, 0:TOK]
                v.tensor_tensor(st, st, r_row, ALU.mult).then_inc(prod_ready, 1)

            def wkv_finish(b, nb):
                if nb is not None:
                    dve.wait_ge(front_filled, nb * NF + USE["s23"] + 1)
                dve.wait_ge(back_filled["bonus"], b + 1)
                ps = back_unit("bonus")
                c_row = ps[:, 0:TOK].unsqueeze(1).to_broadcast([P, SL, TOK])
                v.tensor_tensor(bonus_v[:, :, :], v_sb[:, :, :], c_row, ALU.mult).then_inc(bonus_v_ready, 1)
                dve.wait_ge(reduced, (b + 1) * SL)
                ps = slots(back[1])
                dve.wait_ge(bonus_v_ready, b + 1)
                v.tensor_tensor(y[:, :, :], ps, bonus_v[:, :, :], ALU.add).then_inc(y_ready, 1)

            def back_centre(b):
                dve.wait_ge(back_filled["mean"], b + 1)
                ps = back_unit("mean")
                m_row = ps[:, 0:TOK].unsqueeze(1).to_broadcast([P, SL, TOK])
                v.tensor_tensor(y[:, :, :], y[:, :, :], m_row, ALU.subtract).then_inc(centred, 1)

            def back_scale(b):
                dve.wait_ge(gvar_ready, b + 1)
                v.reciprocal(rstd[:, :], rstd[:, :]).then_inc(grstd_ready, 1)
                dve.wait_ge(sq_ready, b + 1)
                dve.wait_ge(grstd_ready, b + 1)
                r_row = rstd[:, :].unsqueeze(1).to_broadcast([P, SL, TOK])
                v.tensor_tensor(y[:, :, :], y[:, :, :], r_row, ALU.mult).then_inc(normed, 1)

            def back_gate(b):
                dve.wait_ge(affine, (b + 1) * SL)
                v.scalar_tensor_tensor(y[:, :, :], y[:, :, :], 0.5, gate[:, :, :], ALU.mult, ALU.mult).then_inc(gated, 1)

            def back_ln(b):
                dve.wait_ge(back_filled["wo"], b + 1)
                ps = halves(back_unit("wo"))
                dve.wait_ge(res_ready, b + 1)
                v.tensor_tensor(x_res[:, :, :], ps, x_res[:, :, :], ALU.add).then_inc(x1_ready, 1)
                dve.wait_ge(x1_ready, b + 1)
                layer_norm(b, x_res, xn2, stat2_ready, mv2_ready, lvar2_ready, lrstd2_ready, xn2_ready)

            def back_shift(b):
                dve.wait_ge(xc_ready, (b + 1) * (1 + SL))
                v.tensor_tensor(sx2[:, :, :], xc[:, :, 0:TOK], xc[:, :, 1:ROW], ALU.subtract).then_inc(sx2_ready, 1)
                dve.wait_ge(sx2_ready, b + 1)
                for dst, w, s_ready in ((xk2, "ffn_k", xk2_ready), (xr2, "ffn_r", xr2_ready)):
                    for s in range(SL):
                        v.scalar_tensor_tensor(dst[:, s, :], sx2[:, s, :], vecs[w][:, s:s + 1], xc[:, s, 1:ROW], ALU.mult, ALU.add)\
                            .then_inc(s_ready, 1)

            def back_out(b):
                dve.wait_ge(back_filled["fv"], b + 1)
                ps = halves(back_unit("fv"))
                dve.wait_ge(rr_ready, b + 1)
                v.scalar_tensor_tensor(o_sb, o_sb, 1.0, ps, ALU.add, ALU.mult).then_inc(gated_ffn, 1)
                dve.wait_ge(gated_ffn, b + 1)
                v.scalar_tensor_tensor(o_sb, o_sb, 0.5, x_res[:, :, :], ALU.mult, ALU.add).then_inc(out_ready, 1)

            def front1_step(b, c, stored):
                if c == 2: front_scores(b)
                if c == 5: front_normalise(b)
                if c == 7: front_attnT(b, stored)
                if c == 10: front_ln(b)
                if c == 13: front_shift(b)

            def phase2(b, nb):
                front, back_ = nb is not None, b is not None
                if back_: back_centre(b)
                if front: mix(nb, MIX_W); mix(nb, MIX_K)
                if back_: back_scale(b)
                if back_: back_gate(b)
                if front: mix(nb, MIX_V)
                if back_: back_ln(b)
                if front: mix(nb, MIX_R)
                if back_: back_shift(b)
                if front: mix(nb, MIX_G)
                if back_: back_out(b)
                if front: front_gate(nb)

            def phase1(b, nb):
                wkv_bonus(b)
                wkv_kv(b, 0)
                for c in range(NCH):
                    wkv_scan(b, c)
                    if c + 1 < NCH:
                        wkv_kv(b, c + 1)
                    wkv_prod(b, c)
                    if nb is not None:
                        front1_step(nb, c, b if later(b) else None)
                wkv_finish(b, nb)

            v.memset(eps_col[:, :], EPS).then_inc(consts_set, 1)
            v.memset(half_neg[:, :], -0.5).then_inc(consts_set, 1)
            v.memset(decay[:, :, :, 0:1], 0.0).then_inc(consts_set, 1)
            dve.wait_ge(consts_set, 3)
            dve.wait_ge(w_l0, W_L0)
            for c in range(NCH):
                if c == 10: dve.wait_ge(w_mix, W_MIX)
                front1_step(0, c, None)
            phase2(None, 0)
            dve.wait_ge(w_back, W_BACK)
            phase1(0, 1)
            phase2(0, 1)
            with dve.Fori(1, B - 1) as b:
                phase1(b, b + 1)
                phase2(b, b + 1)
            phase1(B - 1, None)
            phase2(B - 1, None)

        @block.scalar
        def _(act):
            a = nc.scalar.activation

            def front_qkv(b):
                act.wait_ge(front_filled, filled(b, "qk"))
                ps = front_unit("qk")
                a(qk[:, 0, :], ps[0:DQ, 0:E], ACT.Identity, bias=bq[:, 0:1]).then_inc(qk_ready, 1)
                a(qk[:, 1, :], ps[0:DQ, E:2 * E], ACT.Identity, bias=bk[:, 0:1]).then_inc(qk_ready, 1)
                act.wait_ge(front_filled, filled(b, "v0"))
                ps = front_unit("v0")
                a(vT[:, :, :].rearrange("p m c -> p (m c)"), ps[:, :], ACT.Copy).then_inc(vT_ready, 1)

            def front_exp(b):
                for use, n0 in (("s01", 0), ("s23", 2)):
                    act.wait_ge(front_filled, filled(b, use))
                    ps = halves(front_unit(use))
                    for n in (n0, n0 + 1):
                        act.wait_ge(max_ready, b * NT + n + 1)
                        ins = a(attn[:, n, :], ps[:, n - n0, :], ACT.Exp, bias=score_max[:, n:n + 1], accum_out=row_sum[:, n:n + 1])
                        ins.then_inc(exp_ready, 1)

            def front_attnT(b, stored):
                if stored is not None:
                    act.wait_ge(out_stored, stored * 16)
                act.wait_ge(front_filled, filled(b, "t01"))
                ps = halves(front_unit("t01"))
                a(attnT[:, 0:2, :], ps, ACT.Copy).then_inc(attnT_act, 1)

            def front_xa(b):
                act.wait_ge(prev_att_landed, (b + 1) * 16 * G)
                if later(b):
                    act.wait_ge(xm_ready, b * NMIX)
                a(xa[:, :, 0], prev_att[:, :], ACT.Copy).then_inc(xa_ready, 1)
                act.wait_ge(front_filled, filled(b, "xnT"))
                ps = slots(front_unit("xnT"))
                for s in range(SL):
                    last = a(xa[:, s, 1:ROW], ps[:, s, :], ACT.Identity, bias=vecs["ln1_b"][:, s:s + 1], scale=vecs["ln1_w"][:, s:s + 1])
                    last.then_inc(xa_ready, 1)

            def front_h(b):
                act.wait_ge(front_filled, filled(b, "w1"))
                ps = front_unit("w1")
                a(h_a[:, :], ps[:, 0:TOK], ACT.Tanh).then_inc(h_ready, 1)
                a(h_b[:, :], ps[DD:DD + DM, E:E + TOK], ACT.Tanh).then_inc(h_ready, 1)

            def td_hidden(b):
                act.wait_ge(front_filled, filled(b, "td1"))
                ps = front_unit("td1")
                a(tw[:, :], ps[0:DD, 0:TOK], ACT.Tanh).then_inc(tw_ready, 1)

            def td_out(b):
                act.wait_ge(front_filled, filled(b, "td2"))
                ps = slots(front_unit("td2"))
                if later(b):
                    act.wait_ge(reduced, b * SL)
                for s in range(SL):
                    a(rate[:, s, :], ps[:, s, :], ACT.Exp, bias=vecs["time_decay"][:, s:s + 1]).then_inc(rate_ready, 1)
                act.wait_ge(rate_ready, (b + 1) * SL)
                if later(b):
                    act.wait_ge(scanned, b * 2 * NCH)
                for s in range(SL):
                    a(decay[:, s, :, 1:ROW], rate[:, s, :].unsqueeze(1).to_broadcast([P, 2, TOK]), ACT.Exp, scale=-1.0).then_inc(decay_ready, 1)

            def evacuate(b, use, dst, ready, former, per):
                act.wait_ge(front_filled, filled(b, use))
                ps = front_unit(use)
                if later(b):
                    act.wait_ge(former, b * per)
                a(dst.rearrange("p s t -> p (s t)"), ps[:, :], ACT.Copy).then_inc(ready, 1)

            def front_th(b):
                act.wait_ge(front_filled, filled(b, "g"))
                ps = front_unit("g")
                if later(b):
                    act.wait_ge(gated, b)
                a(gate[:, :, :].rearrange("p s t -> p (s t)"), ps[:, :], ACT.Tanh, scale=0.5).then_inc(th_ready, 1)

            def save_residual(b):
                act.wait_ge(x_mid_ready, (b + 1) * CT)
                if later(b):
                    act.wait_ge(out_ready, b)
                a(x_res[:, :, :], x_mid[:, :, :], ACT.Copy).then_inc(res_ready, 1)

            def wkv_row0(b, c):
                s, g = divmod(c, G)
                if c == 0:
                    act.wait_ge(front_filled, filled(b, "g"))
                    act.wait_ge(state_landed, (b + 1) * 16 * G)
                    act.wait_ge(decay_ready, (b + 1) * SL)
                if c >= NS:
                    act.wait_ge(reduced, b * SL + (c - NS) // G + 1)
                a(states[:, c % NS, :, 0], state0[:, s * D + g * SL:s * D + (g + 1) * SL], ACT.Copy).then_inc(row0_ready, 1)

            def back_square(b):
                act.wait_ge(centred, b + 1)
                a(sq[:, :, :], y[:, :, :], ACT.Square).then_inc(sq_ready, 1)

            def back_gvar(b):
                act.wait_ge(back_filled["var"], b + 1)
                ps = back_unit("var")
                a(rstd[:, :], ps[:, 0:TOK], ACT.Sqrt, bias=eps_col[:, 0:1]).then_inc(gvar_ready, 1)

            def back_affine(b):
                act.wait_ge(normed, b + 1)
                for s in range(SL):
                    a(y[:, s, :], y[:, s, :], ACT.Identity, bias=vecs["gn_b"][:, s:s + 1], scale=vecs["gn_w"][:, s:s + 1]).then_inc(affine, 1)

            def back_xc(b):
                act.wait_ge(prev_ffn_landed, (b + 1) * 16 * G)
                a(xc[:, :, 0], prev_ffn[:, :], ACT.Copy).then_inc(xc_ready, 1)
                act.wait_ge(back_filled["xcT"], b + 1)
                ps = slots(back_unit("xcT"))
                for s in range(SL):
                    a(xc[:, s, 1:ROW], ps[:, s, :], ACT.Identity, bias=vecs["ln2_b"][:, s:s + 1], scale=vecs["ln2_w"][:, s:s + 1]).then_inc(xc_ready, 1)

            def back_kk(b):
                act.wait_ge(back_filled["fk"], b + 1)
                ps = slots(back_unit("fk"))
                a(kk, ps, ACT.Relu).then_inc(relu_ready, 1)
                act.wait_ge(relu_ready, b + 1)
                a(kk, kk, ACT.Square).then_inc(kk_ready, 1)

            def back_rr(b):
                act.wait_ge(back_filled["fr"], b + 1)
                ps = halves(back_unit("fr"))
                if later(b):
                    act.wait_ge(out_stored, b * 16)
                a(o_sb, ps, ACT.Tanh, scale=0.5).then_inc(rr_ready, 1)

            def front1_step(b, c, stored):
                if c == 0: front_qkv(b)
                if c == 2: front_exp(b)
                if c == 7: front_attnT(b, stored)
                if c == 12: front_xa(b)
                if c == 15: front_h(b)

            def phase2(b, nb):
                front, back_ = nb is not None, b is not None
                if back_: back_square(b)
                if back_: back_gvar(b)
                if front: td_hidden(nb)
                if front: evacuate(nb, "k", k_sb[:, :, :], k_ready, kv_ready, NCH)
                if back_: back_affine(b)
                if front: td_out(nb)
                if front: evacuate(nb, "v", v_sb[:, :, :], v_ready, bonus_v_ready, 1)
                if back_: back_xc(b)
                if front: evacuate(nb, "r", r_sb[:, :, :], r_ready, prod_ready, NCH)
                if front:
                    for g in range(G):
                        evacuate(nb, f"rep{g}", vrep[:, g, :, :], vrep_ready, kv_ready, NCH)
                if back_: back_kk(b); back_rr(b)
                if front: front_th(nb)
                if front: save_residual(nb)

            def phase1(b, nb):
                for c in range(NS):
                    wkv_row0(b, c)
                for c in range(NCH):
                    if c % G == G - 1:
                        for n in range(c + 1 - G + NS, min(c + 1 + NS, NCH)):
                            wkv_row0(b, n)
                    if nb is not None:
                        front1_step(nb, c, b if later(b) else None)

            act.wait_ge(consts_set, 3)
            act.wait_ge(w_l0, W_L0)
            for c in range(NCH):
                if c == 12: act.wait_ge(w_mix, W_MIX)
                front1_step(0, c, None)
            phase2(None, 0)
            act.wait_ge(w_back, W_BACK)
            phase1(0, 1)
            phase2(0, 1)
            with act.Fori(1, B - 1) as b:
                phase1(b, b + 1)
                phase2(b, b + 1)
            phase1(B - 1, None)
            phase2(B - 1, None)

        @block.gpsimd
        def _(pool):
            g_ = nc.gpsimd

            def ln_power(b, lvar_s, lrstd_s):
                pool.wait_ge(lvar_s, b + 1)
                g_.tensor_tensor(ln_rstd[:, :], ln_var[:, :], half_neg[:, 0:1].to_broadcast([P, CT]), ALU.pow).then_inc(lrstd_s, 1)

            def mix_add(b, n):
                pool.wait_ge(mixed, b * NMIX + n + 1)
                g_.tensor_tensor(xm[n % 2], xm[n % 2], xa[:, :, 1:ROW], ALU.add).then_inc(xm_ready, 1)

            def store(b):
                pool.wait_ge(out_ready, b + 1)
                pool.dma_start(out_dram[b, :, :].rearrange("(c p) n -> p c n", p=P), o_sb).then_inc(out_stored, 16)

            def phase2(b, nb):
                front, back_ = nb is not None, b is not None
                if front: mix_add(nb, 0); mix_add(nb, 1)
                if front: mix_add(nb, 2)
                if back_: ln_power(b, lvar2_ready, lrstd2_ready)
                if front: mix_add(nb, 3)
                if front: mix_add(nb, 4)
                if back_: store(b)

            def phase1(b, nb):
                if nb is not None:
                    ln_power(nb, lvar_ready, lrstd_ready)

            pool.wait_ge(consts_set, 3)
            ln_power(0, lvar_ready, lrstd_ready)
            phase2(None, 0)
            phase1(0, 1)
            phase2(0, 1)
            with pool.Fori(1, B - 1) as b:
                phase1(b, b + 1)
                phase2(b, b + 1)
            phase1(B - 1, None)
            phase2(B - 1, None)


def kernel(**inputs):
    import numpy as np
    import concourse.bacc as bacc
    from concourse import mybir as _mybir
    from concourse.bass_utils import run_bass_kernel_spmd as run

    def t(name):
        return np.asarray(inputs[name])

    def channels(w, axis):
        shape = w.shape
        w = w.reshape(shape[:axis] + (H, G, SL) + shape[axis + 1:]).swapaxes(axis, axis + 1)
        return w.reshape(shape[:axis] + (P, SL) + shape[axis + 1:])

    def proj(name):
        return channels(channels(t(name).T, 1), 0).swapaxes(2, 3)

    pre0, pre1 = "L0_xattn_", "L1_xattn_"
    part = np.arange(P)
    rep = np.zeros((P, G, P), np.float32)
    for g in range(G):
        rep[H * g + part % H, g, part] = 1.0
    same_head = (part[:, None] % H == part[None, :] % H).astype(np.float32)
    arrays = {
        "x": t("x"), "ctx": t("ctx_2048"),
        "wq": t(pre0 + "Wq").T.reshape(CT, P, DQ).transpose(1, 0, 2),
        "wk": t(pre0 + "Wk").T.reshape(CT, P, DQ).transpose(1, 0, 2),
        "wv": t(pre0 + "Wv").T.reshape(CT, P, TOK).transpose(1, 0, 2),
        "bq": t(pre0 + "bq").reshape(DQ, 1), "bk": t(pre0 + "bk").reshape(DQ, 1),
        "bv": t(pre0 + "bv").reshape(CT, P).T,
        "ident": np.eye(P, dtype=np.float32), "rep": rep, "red": same_head[:, 0:H],
        "head_sum": same_head, "head_mean": same_head * np.float32(1.0 / D),
        "maa_stack": channels(t(pre1 + "maa_stack").reshape(NMIX, E), 1).transpose(1, 0, 2),
        "maa_w1": channels(t(pre1 + "maa_w1"), 0),
        "maa_w2": channels(t(pre1 + "maa_w2").reshape(NMIX * DM, E), 1).transpose(0, 2, 1),
        "td_w1": channels(t(pre1 + "td_w1"), 0),
        "td_w2": channels(t(pre1 + "td_w2"), 1).transpose(0, 2, 1),
        "ffn_k": channels(t(pre1 + "ffn_maa_k"), 0), "ffn_r": channels(t(pre1 + "ffn_maa_r"), 0),
        "Wo": channels(t(pre1 + "Wo").T, 0), "Wfr": channels(t(pre1 + "Wfr").T, 0), "Wfv": channels(t(pre1 + "Wfv").T, 0),
    }
    for n in ["ln1_w", "ln1_b", "maa_x", "time_decay", "u", "gn_w", "gn_b", "ln2_w", "ln2_b"]:
        arrays[n] = channels(t(pre1 + n).reshape(E), 0)
    for n in ["Wr", "Wk", "Wv", "Wg", "Wfk"]:
        arrays[n] = proj(pre1 + n)

    nc = bacc.Bacc("TRN2", target_bir_lowering=False, num_devices=1)
    io, given = {}, {}
    for n in _INS:
        arr = np.ascontiguousarray(arrays[n])
        given[f"in_{n}"] = arr
        io[n] = nc.dram_tensor(f"in_{n}", arr.shape, _mybir.dt.from_np(arr.dtype), kind="ExternalInput").ap()
    out = nc.dram_tensor("out", (B, TOK, E), _mybir.dt.float32, kind="ExternalOutput").ap()
    xattn_rwkv_kernel(nc, io, out)
    result = run(nc, [given], core_ids=[0])
    return result.results[0]["out"]
```

```python
from contextlib import ExitStack

import concourse.bass as bass
from concourse import mybir

ALU = mybir.AluOpType
ACT = mybir.ActivationFunctionType
AX_X = mybir.AxisListType.X
F32 = mybir.dt.float32

P = 128
B, TOK, E = 8, 256, 512
CT = TOK // P
NT = E // P
DQ = 32
H, D = 32, 16
SL = E // P
G = D // SL
DM, DD = 32, 64
NMIX = 5
MIX_K, MIX_W, MIX_V, MIX_R, MIX_G = range(NMIX)
MIX_ORDER = [MIX_V, MIX_W, MIX_K, MIX_R, MIX_G]
ROW = TOK + 1
NCH = G * SL
AHEAD = 3
NS = 7
EPS = 1e-5

FRONT_USES = ["qk", "v0", "s01", "s23", "t01", "t23", "out", "g", "xnT", "w1",
              "m2", "m1", "v", "m0", "td1", "m3", "k", "td2", "m4", "r"]
NF = len(FRONT_USES)
USE = {n: i for i, n in enumerate(FRONT_USES)}

_INS = ["x", "ctx", "wq", "wk", "wv", "bq", "bk", "bv", "ident", "red", "head_sum", "head_mean",
        "ln1_w", "ln1_b", "maa_x", "maa_stack", "maa_w1", "maa_w2", "td_w1", "td_w2", "time_decay", "u",
        "Wr", "Wk", "Wv", "Wg", "Wo", "gn_w", "gn_b", "ln2_w", "ln2_b", "ffn_k", "ffn_r", "Wfk", "Wfr", "Wfv"]


def xattn_rwkv_kernel(nc, io, out_dram):
    with ExitStack() as ctx:
        def sb(name, *shape):
            return ctx.enter_context(nc.sbuf_tensor(name, list(shape), F32))

        def psum(name, *shape):
            return ctx.enter_context(nc.psum_tensor(name, list(shape), F32))

        def sem(name):
            return ctx.enter_context(nc.semaphore(name))

        wq, wk = sb("wq", P, CT, DQ), sb("wk", P, CT, DQ)
        wv = sb("wv", P, CT, TOK)
        bq, bk, bv = sb("bq", DQ, 1), sb("bk", DQ, 1), sb("bv", P, CT)
        ident = sb("ident", P, P)
        red = sb("red", P, H)
        head_sum, head_mean = sb("head_sum", P, P), sb("head_mean", P, P)
        vecs = {n: sb(n, P, SL) for n in ["ln1_w", "ln1_b", "maa_x", "time_decay", "u", "gn_w", "gn_b",
                                          "ln2_w", "ln2_b", "ffn_k", "ffn_r"]}
        maa_stack = sb("maa_stack", P, NMIX, SL)
        maa_w1 = sb("maa_w1", P, SL, NMIX * DM)
        maa_w2a = sb("maa_w2a", P, SL, P)
        low_rank = sb("low_rank", DD + DM, SL, P)
        td_w2, maa_w2b = low_rank[0:DD], low_rank[DD:DD + DM]
        td_w1 = sb("td_w1", P, SL, DD)
        w_proj = {n: sb(n, P, SL, SL, P) for n in ["Wr", "Wk", "Wv", "Wg", "Wfk"]}
        w_tok = {n: sb(n, P, SL, E) for n in ["Wo", "Wfr", "Wfv"]}
        wait_col = sb("wait_col", P, 1)
        eps_col = sb("eps_col", P, 1)
        half_neg = sb("half_neg", P, 1)

        x_in, ctx_in = sb("x_in", P, CT, E), sb("ctx_in", P, CT, E)
        prev_att, prev_ffn = sb("prev_att", P, SL), sb("prev_ffn", P, SL)
        state0 = sb("state0", P, SL * D)
        reg_a = sb("reg_a", P, NT, E)
        reg_b = sb("reg_b", P, NT, E)
        reg_c = sb("reg_c", P, NT, TOK)
        reg_d = sb("reg_d", P, 2, E)
        x_mid, x_res = sb("x_mid", P, CT, E), sb("x_res", P, CT, E)
        xa, xc = sb("xa", P, SL, ROW), sb("xc", P, SL, ROW)
        sx = sb("sx", P, SL, TOK)
        h_a = sb("h_a", P, TOK)
        low_act = sb("low_act", DD + DM, TOK)
        tw, h_b = low_act[0:DD], low_act[DD:DD + DM]
        decay = sb("decay", P, SL, 2, ROW)
        vrep = sb("vrep", P, G, SL, TOK)
        k_sb, v_sb, r_sb, gate = (sb(n, P, SL, TOK) for n in ["k_sb", "v_sb", "r_sb", "gate"])
        states = sb("states", P, NS, SL, ROW)
        y = sb("y", P, SL, TOK)
        rstd = sb("rstd", P, TOK)
        score_max, row_sum, row_inv = sb("score_max", P, NT), sb("row_sum", P, NT), sb("row_inv", P, NT)
        ln_stat, ln_mv, ln_var, ln_rstd = sb("ln_stat", P, CT, 6), sb("ln_mv", P, CT, 2), sb("ln_var", P, CT), sb("ln_rstd", P, CT)

        attn, attnT = reg_a, reg_b
        xn = reg_a[:, 0:2, :]
        xpre = reg_a[:, 2:4, :].rearrange("p a (c t) -> p (a c) t", t=TOK)
        xk2 = reg_a[:, 0:2, :].rearrange("p a (c t) -> p (a c) t", t=TOK)
        xr2 = xpre
        kk = reg_b[:, 0:2, :].rearrange("p a (c t) -> p (a c) t", t=TOK)
        o_sb = reg_b[:, 2:4, :]
        vT = reg_c
        xn2 = reg_c[:, :, :].rearrange("p (c a) t -> p c (a t)", c=CT)
        sx2 = reg_c
        qk = reg_d[0:DQ, :, :]
        sq = reg_d[:, :, :].rearrange("p a (c t) -> p (a c) t", t=TOK)
        bonus = y
        rate = gate[:, :, :]
        xm = [states[:, n, :, 0:TOK] for n in (2, 3, 4, 5)] + [sx[:, :, :]]

        front = [psum("front0", P, 1024), psum("front1", P, 1024)]
        back = [psum("back0", P, 1024), psum("back1", P, 1024)]

        def slots(ps):
            return ps[:, :].rearrange("p (s t) -> p s t", t=TOK)

        def halves(ps):
            return ps[:, :].rearrange("p (c n) -> p c n", c=2)

        w_l0, w_mix, w_wkv, w_back = sem("w_l0"), sem("w_mix"), sem("w_wkv"), sem("w_back")
        x_landed, ctx_landed, prev_att_landed = sem("x_landed"), sem("ctx_landed"), sem("prev_att_landed")
        prev_ffn_landed, state_landed, out_stored = sem("prev_ffn_landed"), sem("state_landed"), sem("out_stored")
        consts_set = sem("consts_set")
        front_filled = sem("front_filled")
        back_filled = {u: sem(f"{u}_filled") for u in ["bonus", "xcT", "fk", "fr", "fv", "mean", "wo", "var"]}
        qk_ready = sem("qk_ready")
        vT_ready = sem("vT_ready")
        max_ready = sem("max_ready")
        exp_ready = sem("exp_ready")
        inv_ready = sem("inv_ready")
        attn_ready = sem("attn_ready")
        attnT_ready = sem("attnT_ready")
        x_mid_ready = sem("x_mid_ready")
        stat_ready = sem("stat_ready")
        mv_ready = sem("mv_ready")
        lvar_ready = sem("lvar_ready")
        lrstd_ready = sem("lrstd_ready")
        xn_ready = sem("xn_ready")
        xa_ready = sem("xa_ready")
        sx_ready = sem("sx_ready")
        xpre_ready = sem("xpre_ready")
        h_ready = sem("h_ready")
        mixed = sem("mixed")
        xm_ready = sem("xm_ready")
        tw_ready = sem("tw_ready")
        rate_ready = sem("rate_ready")
        decay_ready = sem("decay_ready")
        k_ready, v_ready, r_ready = sem("k_ready"), sem("v_ready"), sem("r_ready")
        vrep_landed = sem("vrep_landed")
        th_ready, gate_ready = sem("th_ready"), sem("gate_ready")
        res_ready = sem("res_ready")
        bonus_ready = sem("bonus_ready")
        kv_ready, row0_ready, scanned = sem("kv_ready"), sem("row0_ready"), sem("scanned")
        prod_ready, reduced = sem("prod_ready"), sem("reduced")
        bonus_v_ready, y_ready = sem("bonus_v_ready"), sem("y_ready")
        centred, sq_ready, gvar_ready, grstd_ready = sem("centred"), sem("sq_ready"), sem("gvar_ready"), sem("grstd_ready")
        normed, affine, gated = sem("normed"), sem("affine"), sem("gated")
        x1_ready = sem("x1_ready")
        stat2_ready, mv2_ready, lvar2_ready, lrstd2_ready = sem("stat2_ready"), sem("mv2_ready"), sem("lvar2_ready"), sem("lrstd2_ready")
        xn2_ready = sem("xn2_ready")
        xc_ready = sem("xc_ready")
        sx2_ready, xk2_ready, xr2_ready = sem("sx2_ready"), sem("xk2_ready"), sem("xr2_ready")
        relu_ready, kk_ready = sem("relu_ready"), sem("kk_ready")
        rr_ready, gated_ffn, out_ready = sem("rr_ready"), sem("gated_ffn"), sem("out_ready")

        block = ctx.enter_context(nc.Block())

        def later(b):
            return not (isinstance(b, int) and b == 0)

        def buf(c):
            return (c + NS - 1) % NS

        def filled(b, use):
            if isinstance(b, int) and b == 0 and USE[use] < USE["g"]:
                return USE[use] + 1
            if isinstance(b, int) and b == B:
                return B * NF
            return b * NF + USE[use]

        def front_unit(use):
            return front[USE[use] % 2]

        FRONT_DRAINED = {
            "qk": (qk_ready, 2, 2), "v0": (vT_ready, 1, 1), "s01": (exp_ready, NT, 2), "s23": (exp_ready, NT, NT),
            "t01": (attnT_ready, 2, 1), "t23": (attnT_ready, 2, 2), "out": (x_mid_ready, CT, CT), "xnT": (xa_ready, 1 + SL, 1 + SL),
            "w1": (h_ready, 2, 2), "td1": (tw_ready, 1, 1), "td2": (rate_ready, SL, SL),
            "k": (k_ready, 1, 1), "v": (v_ready, 1, 1), "r": (r_ready, 1, 1), "g": (gate_ready, 1, 0)}
        FRONT_DRAINED.update({f"m{f}": (mixed, NMIX, n + 1) for n, f in enumerate(MIX_ORDER)})
        def has_former(b, use):
            return later(b) or USE[use] >= 2

        def former_drained(b, use):
            before = USE[use] - 2
            if isinstance(b, int) and b == 0 and FRONT_USES[before] == "g":
                before -= 2
            if isinstance(b, int) and b == B:
                before = USE["r"] - NF
            s, per, n = FRONT_DRAINED[FRONT_USES[before % NF]]
            return (s, b * per + n) if before >= 0 else (s, b * per)

        back0, back1 = back

        @block.sync
        def _(sp):
            def load(dst, name, s):
                sp.dma_start(dst, io[name]).then_inc(s, 16)

            def by_group(row, n):
                return row.rearrange("(h g n) -> g h n", g=G, n=n)

            def load_inputs(b):
                if later(b):
                    sp.wait_ge(x_mid_ready, b * CT)
                sp.dma_start(x_in[:, :, :], io["x"][b, :, :].rearrange("(c p) n -> p c n", p=P)).then_inc(x_landed, 16)
                sp.dma_start(ctx_in[:, :, :], io["ctx"][b, :, :].rearrange("(c p) n -> p c n", p=P)).then_inc(ctx_landed, 16)
                if later(b):
                    sp.wait_ge(xa_ready, b * (1 + SL))
                for g in range(G):
                    sp.dma_start(prev_att[H * g:H * (g + 1), :], by_group(io["ctx"][b, 1, :], SL)[g]).then_inc(prev_att_landed, 16)

            def load_state(b):
                if later(b):
                    sp.wait_ge(row0_ready, b * NCH)
                for g in range(G):
                    sp.dma_start(state0[H * g:H * (g + 1), :], by_group(io["ctx"][b, 2:2 + D, :].rearrange("r e -> (r e)"), SL * D)[g])\
                        .then_inc(state_landed, 16)

            def load_prev_ffn(b):
                if later(b):
                    sp.wait_ge(xc_ready, b * (1 + SL))
                for g in range(G):
                    sp.dma_start(prev_ffn[H * g:H * (g + 1), :], by_group(io["ctx"][b, 0, :], SL)[g]).then_inc(prev_ffn_landed, 16)

            def replicate(b):
                sp.wait_ge(v_ready, b + 1)
                if later(b):
                    sp.wait_ge(kv_ready, b * NCH)
                for g in range(G):
                    for to in range(G):
                        sp.dma_start(vrep[H * to:H * (to + 1), g, :, :], v_sb[H * g:H * (g + 1), :, :]).then_inc(vrep_landed, 16)

            for name, dst in [("wq", wq), ("wk", wk), ("bq", bq), ("bk", bk)]:
                load(dst[:], name, w_l0)
            load_inputs(0)
            load_state(0)
            load_prev_ffn(0)
            for name, dst in [("wv", wv), ("bv", bv), ("ident", ident)]:
                load(dst[:], name, w_l0)
            for name in ["ln1_w", "ln1_b", "maa_x", "time_decay", "u"]:
                load(vecs[name][:], name, w_mix)
            load(maa_stack[:], "maa_stack", w_mix)
            load(maa_w1[:], "maa_w1", w_mix)
            sp.dma_start(maa_w2a[:], io["maa_w2"][0:P, :, :]).then_inc(w_mix, 16)
            sp.dma_start(maa_w2b[:], io["maa_w2"][P:P + DM, :, :]).then_inc(w_mix, 16)
            load(td_w1[:], "td_w1", w_mix)
            load(td_w2[:], "td_w2", w_mix)
            for name in ["Wk", "Wv", "Wr", "Wg"]:
                load(w_proj[name][:], name, w_wkv)
            for name, dst in [("red", red), ("head_sum", head_sum)]:
                load(dst[:], name, w_wkv)
            load(head_mean[:], "head_mean", w_back)
            for name in ["gn_w", "gn_b", "ln2_w", "ln2_b", "ffn_k", "ffn_r"]:
                load(vecs[name][:], name, w_back)
            for name in ["Wo", "Wfr", "Wfv"]:
                load(w_tok[name][:], name, w_back)
            load(w_proj["Wfk"][:], "Wfk", w_back)
            replicate(0)
            load_inputs(1)
            load_state(1)
            with sp.Fori(2, B) as b:
                replicate(b - 1)
                load_inputs(b)
                load_prev_ffn(b - 1)
                load_state(b)
            replicate(B - 1)
            load_prev_ffn(B - 1)
            sp.wait_ge(out_stored, 16 * B)

        W_L0, W_MIX, W_WKV, W_BACK = 16 * 7, 16 * 11, 16 * 6, 16 * 11

        @block.tensor
        def _(pe):
            mm = nc.tensor.matmul

            def front_qk(b):
                pe.wait_ge(x_landed, (b + 1) * 16)
                pe.wait_ge(ctx_landed, (b + 1) * 16)
                if has_former(b, "qk"):
                    pe.wait_ge(*former_drained(b, "qk"))
                ps = front_unit("qk")
                for half, w, src in ((0, wq, x_in), (1, wk, ctx_in)):
                    for c in range(CT):
                        last = mm(ps[0:DQ, half * E:(half + 1) * E], w[:, c, :], src[:, c, :], start=(c == 0), stop=(c == CT - 1))
                last.then_inc(front_filled, 1)

            def front_v0(b):
                pe.wait_ge(ctx_landed, (b + 1) * 16)
                if has_former(b, "v0"):
                    pe.wait_ge(*former_drained(b, "v0"))
                ps = slots(front_unit("v0"))
                for m in range(NT):
                    for c in range(CT):
                        last = mm(ps[:, m, :], ctx_in[:, c, m * P:(m + 1) * P], wv[:, c, :], start=(c == 0), stop=(c == CT - 1))
                last.then_inc(front_filled, 1)

            def front_scores(b):
                pe.wait_ge(qk_ready, (b + 1) * 2)
                for use, n0 in (("s01", 0), ("s23", 2)):
                    if has_former(b, use):
                        pe.wait_ge(*former_drained(b, use))
                    ps = halves(front_unit(use))
                    for n in (n0, n0 + 1):
                        last = mm(ps[:, n - n0, :], qk[:, 0, n * P:(n + 1) * P], qk[:, 1, :], start=True, stop=True)
                    last.then_inc(front_filled, 1)

            def front_transposes(b):
                pe.wait_ge(attn_ready, (b + 1) * NT)
                for use, m0 in (("t01", 0), ("t23", 2)):
                    if has_former(b, use):
                        pe.wait_ge(*former_drained(b, use))
                    ps = halves(front_unit(use))
                    for m in (m0, m0 + 1):
                        for n in range(NT):
                            last = nc.tensor.transpose(ps[:, m - m0, n * P:(n + 1) * P], attn[:, n, m * P:(m + 1) * P], ident[:, :])
                    last.then_inc(front_filled, 1)

            def front_out(b):
                pe.wait_ge(vT_ready, b + 1)
                pe.wait_ge(attnT_ready, (b + 1) * 2)
                if has_former(b, "out"):
                    pe.wait_ge(*former_drained(b, "out"))
                ps = halves(front_unit("out"))
                for c in range(CT):
                    for m in range(NT):
                        last = mm(ps[:, c, :], vT[:, m, c * P:(c + 1) * P], attnT[:, m, :], start=(m == 0), stop=(m == NT - 1))
                last.then_inc(front_filled, 1)

            def front_xnT(b):
                pe.wait_ge(xn_ready, (b + 1) * CT)
                if has_former(b, "xnT"):
                    pe.wait_ge(*former_drained(b, "xnT"))
                ps = slots(front_unit("xnT"))
                for s in range(SL):
                    for c in range(CT):
                        last = nc.tensor.transpose(ps[:, s, c * P:(c + 1) * P], xn[:, c, s * P:(s + 1) * P], ident[:, :])
                last.then_inc(front_filled, 1)

            def front_w1(b):
                pe.wait_ge(xpre_ready, (b + 1) * SL)
                if has_former(b, "w1"):
                    pe.wait_ge(*former_drained(b, "w1"))
                ps = front_unit("w1")
                for lo, hi, p0, off in ((0, P, 0, 0), (P, NMIX * DM, DD, E)):
                    for s in range(SL):
                        last = mm(ps[p0:p0 + hi - lo, off:off + TOK], maa_w1[:, s, lo:hi], xpre[:, s, :], start=(s == 0), stop=(s == SL - 1))
                last.then_inc(front_filled, 1)

            def mix(b, f):
                if f == MIX_ORDER[0]:
                    pe.wait_ge(h_ready, (b + 1) * 2)
                if has_former(b, f"m{f}"):
                    pe.wait_ge(*former_drained(b, f"m{f}"))
                ps = slots(front_unit(f"m{f}"))
                lo = f * DM % P
                w2, h = (maa_w2a, h_a) if f * DM < P else (maa_w2b, h_b)
                for s in range(SL):
                    last = mm(ps[:, s, :], w2[lo:lo + DM, s, :], h[lo:lo + DM, :], start=True, stop=True)
                last.then_inc(front_filled, 1)

            def project(b, use, w, f):
                n = MIX_ORDER.index(f)
                cycle = b + 1 if use == "g" else b
                pe.wait_ge(xm_ready, b * NMIX + n + 1)
                pe.wait_ge(*former_drained(cycle, use))
                ps = slots(front_unit(use))
                for o in range(SL):
                    for s in range(SL):
                        last = mm(ps[:, o, :], w[:, s, o, :], xm[n][:, s, :], start=(s == 0), stop=(s == SL - 1))
                last.then_inc(front_filled, 1)

            def td_hidden(b):
                pe.wait_ge(xm_ready, b * NMIX + 2)
                if has_former(b, "td1"):
                    pe.wait_ge(*former_drained(b, "td1"))
                ps = front_unit("td1")
                for s in range(SL):
                    last = mm(ps[0:DD, 0:TOK], td_w1[:, s, :], xm[1][:, s, :], start=(s == 0), stop=(s == SL - 1))
                last.then_inc(front_filled, 1)

            def td_out(b):
                pe.wait_ge(tw_ready, b + 1)
                if has_former(b, "td2"):
                    pe.wait_ge(*former_drained(b, "td2"))
                ps = slots(front_unit("td2"))
                for s in range(SL):
                    last = mm(ps[:, s, :], td_w2[:, s, :], tw[:, :], start=True, stop=True)
                last.then_inc(front_filled, 1)

            def wkv_bonus(b):
                pe.wait_ge(bonus_ready, (b + 1) * SL)
                if later(b):
                    pe.wait_ge(x1_ready, b)
                for s in range(SL):
                    last = mm(back0[:, 0:TOK], head_sum[:, :], bonus[:, s, :], start=(s == 0), stop=(s == SL - 1))
                last.then_inc(back_filled["bonus"], 1)

            def wkv_reduce(b, s):
                pe.wait_ge(prod_ready, b * NCH + G * (s + 1))
                if s == 0 and later(b):
                    pe.wait_ge(xc_ready, b * (1 + SL))
                for half in range(2):
                    for g in range(G):
                        chunk = states[:, buf(s * G + g), 2 * half:2 * half + 2, 0:TOK]
                        last = mm(back1[H * g:H * (g + 1), half * 2 * TOK:(half + 1) * 2 * TOK], red[:, :], chunk,
                                  start=(s == 0), stop=(s == SL - 1))
                last.then_inc(reduced, 1)

            def tok_product(ps, x, w):
                for c in range(CT):
                    for s in range(SL):
                        last = mm(halves(ps)[:, c, :], x[:, s, c * P:(c + 1) * P], w[:, s, :], start=(s == 0), stop=(s == SL - 1))
                return last

            def back_mean(b):
                pe.wait_ge(y_ready, b + 1)
                if later(b):
                    pe.wait_ge(gated_ffn, b)
                for s in range(SL):
                    last = mm(back0[:, 0:TOK], head_mean[:, :], y[:, s, :], start=(s == 0), stop=(s == SL - 1))
                last.then_inc(back_filled["mean"], 1)

            def back_var(b):
                pe.wait_ge(sq_ready, b + 1)
                for s in range(SL):
                    last = mm(back1[:, 0:TOK], head_mean[:, :], sq[:, s, :], start=(s == 0), stop=(s == SL - 1))
                last.then_inc(back_filled["var"], 1)

            def back_wo(b):
                pe.wait_ge(gated, b + 1)
                tok_product(back0, y, w_tok["Wo"]).then_inc(back_filled["wo"], 1)

            def back_xcT(b):
                pe.wait_ge(xn2_ready, (b + 1) * CT)
                for s in range(SL):
                    for c in range(CT):
                        last = nc.tensor.transpose(slots(back1)[:, s, c * P:(c + 1) * P], xn2[:, c, s * P:(s + 1) * P], ident[:, :])
                last.then_inc(back_filled["xcT"], 1)

            def back_fk(b, last_one=False):
                pe.wait_ge(xk2_ready, (b + 1) * SL)
                if not last_one:
                    pe.wait_ge(bonus_v_ready, b + 2)
                for o in range(SL):
                    for s in range(SL):
                        last = mm(slots(back0)[:, o, :], w_proj["Wfk"][:, s, o, :], xk2[:, s, :], start=(s == 0), stop=(s == SL - 1))
                last.then_inc(back_filled["fk"], 1)

            def back_fr(b):
                pe.wait_ge(xr2_ready, (b + 1) * SL)
                pe.wait_ge(relu_ready, b + 1)
                tok_product(back0, xr2, w_tok["Wfr"]).then_inc(back_filled["fr"], 1)

            def back_fv(b):
                pe.wait_ge(kk_ready, b + 1)
                pe.wait_ge(rr_ready, b + 1)
                tok_product(back0, kk, w_tok["Wfv"]).then_inc(back_filled["fv"], 1)

            def phase_a(b, tail, nb):
                if tail is not None: back_xcT(tail)
                if nb is not None: front_qk(nb)
                wkv_bonus(b)
                if nb is not None: front_v0(nb)
                if tail is not None: back_fk(tail)
                if tail is not None: back_fr(tail)
                wkv_reduce(b, 0)
                if nb is not None: front_scores(nb)
                if tail is not None: back_fv(tail)
                if nb is not None: front_transposes(nb)
                wkv_reduce(b, 1)
                if nb is not None: front_out(nb)
                project(b, "g", w_proj["Wg"], MIX_G)
                if nb is not None: front_xnT(nb)
                wkv_reduce(b, 2)
                if nb is not None:
                    front_w1(nb)
                    mix(nb, MIX_V)
                    mix(nb, MIX_W)
                wkv_reduce(b, 3)

            def phase_b(b, nb):
                if nb is not None: project(nb, "v", w_proj["Wv"], MIX_V)
                if b is not None: back_mean(b)
                if nb is not None:
                    mix(nb, MIX_K)
                    td_hidden(nb)
                    mix(nb, MIX_R)
                if b is not None: back_var(b)
                if nb is not None:
                    project(nb, "k", w_proj["Wk"], MIX_K)
                    td_out(nb)
                    mix(nb, MIX_G)
                if b is not None: back_wo(b)
                if nb is not None: project(nb, "r", w_proj["Wr"], MIX_R)

            pe.wait_ge(w_l0, W_L0)
            front_qk(0)
            front_v0(0)
            front_scores(0)
            front_transposes(0)
            front_out(0)
            front_xnT(0)
            pe.wait_ge(w_mix, W_MIX)
            front_w1(0)
            mix(0, MIX_V)
            mix(0, MIX_W)
            pe.wait_ge(w_wkv, W_WKV)
            phase_b(None, 0)
            pe.wait_ge(w_back, W_BACK)
            phase_a(0, None, 1)
            phase_b(0, 1)
            with pe.Fori(1, B - 1) as b:
                phase_a(b, b - 1, b + 1)
                phase_b(b, b + 1)
            phase_a(B - 1, B - 2, None)
            phase_b(B - 1, None)
            back_xcT(B - 1)
            back_fk(B - 1, last_one=True)
            back_fr(B - 1)
            back_fv(B - 1)

        @block.vector
        def _(dve):
            v = nc.vector

            def front_scores(b):
                for use, n0 in (("s01", 0), ("s23", 2)):
                    dve.wait_ge(front_filled, filled(b, use))
                    ps = halves(front_unit(use))
                    for n in (n0, n0 + 1):
                        if later(b):
                            dve.wait_ge(attn_ready, b * NT)
                        v.tensor_reduce(score_max[:, n:n + 1], ps[:, n - n0, :], AX_X, ALU.max, negate=True).then_inc(max_ready, 1)

            def layer_norm(b, x, dst, stat_s, mv_s, lvar_s, lrstd_s, out_s):
                for c in range(CT):
                    v.bn_stats(ln_stat[:, c, :], x[:, c, :]).then_inc(stat_s, 1)
                dve.wait_ge(stat_s, (b + 1) * CT)
                v.memset(wait_col[:, :], 0.0)
                for c in range(CT):
                    v.bn_aggr(ln_mv[:, c, :], ln_stat[:, c, :]).then_inc(mv_s, 1)
                dve.wait_ge(mv_s, (b + 1) * CT)
                v.tensor_scalar(ln_var[:, :], ln_mv[:, :, 1], EPS, None, ALU.add).then_inc(lvar_s, 1)
                dve.wait_ge(lrstd_s, b + 1)
                for c in range(CT):
                    v.tensor_scalar(dst[:, c, :].rearrange("p (s g h) -> p h g s", s=SL, g=G),
                                    x[:, c, :].rearrange("p (h g s) -> p h g s", s=SL, g=G), ln_mv[:, c, 0:1], ln_rstd[:, c:c + 1], ALU.subtract, ALU.mult).then_inc(out_s, 1)

            def front_inverse(b):
                dve.wait_ge(exp_ready, (b + 1) * NT)
                for n in range(NT):
                    v.reciprocal(row_inv[:, n:n + 1], row_sum[:, n:n + 1]).then_inc(inv_ready, 1)

            def front_ln(b):
                dve.wait_ge(front_filled, filled(b, "out"))
                ps = halves(front_unit("out"))
                if later(b):
                    dve.wait_ge(res_ready, b)
                for c in range(CT):
                    ins = v.scalar_tensor_tensor(x_mid[:, c, :], ps[:, c, :], bv[:, c:c + 1], x_in[:, c, :], ALU.add, ALU.add)
                    ins.then_inc(x_mid_ready, 1)
                dve.wait_ge(x_mid_ready, (b + 1) * CT)
                layer_norm(b, x_mid, xn, stat_ready, mv_ready, lvar_ready, lrstd_ready, xn_ready)

            def front_shift(b):
                dve.wait_ge(xa_ready, (b + 1) * (1 + SL))
                if later(b):
                    dve.wait_ge(front_filled, filled(b, "g"))
                v.tensor_tensor(sx[:, :, :], xa[:, :, 0:TOK], xa[:, :, 1:ROW], ALU.subtract).then_inc(sx_ready, 1)
                dve.wait_ge(sx_ready, b + 1)
                for s in range(SL):
                    v.scalar_tensor_tensor(xpre[:, s, :], sx[:, s, :], vecs["maa_x"][:, s:s + 1], xa[:, s, 1:ROW], ALU.mult, ALU.add)\
                        .then_inc(xpre_ready, 1)

            def mix(b, f):
                n = MIX_ORDER.index(f)
                dve.wait_ge(front_filled, filled(b, f"m{f}"))
                ps = slots(front_unit(f"m{f}"))
                if later(b) and n < 2:
                    dve.wait_ge(reduced, b * SL - 1)
                elif later(b) and n < 4:
                    dve.wait_ge(reduced, b * SL)
                elif n == 4:
                    dve.wait_ge(mixed, b * NMIX + 4)
                for s in range(SL):
                    last = v.scalar_tensor_tensor(xm[n][:, s, :], ps[:, s, :], maa_stack[:, f, s:s + 1], sx[:, s, :], ALU.add, ALU.mult)
                last.then_inc(mixed, 1)

            def front_gate(b):
                dve.wait_ge(front_filled, filled(b + 1, "g"))
                ps = front_unit("g")
                dve.wait_ge(th_ready, b + 1)
                g2 = gate[:, :, :].rearrange("p s t -> p (s t)")
                v.scalar_tensor_tensor(g2, g2, 1.0, ps[:, :], ALU.add, ALU.mult).then_inc(gate_ready, 1)

            def wkv_bonus(b):
                dve.wait_ge(k_ready, b + 1)
                dve.wait_ge(r_ready, b + 1)
                if later(b):
                    dve.wait_ge(back_filled["wo"], b)
                for s in range(SL):
                    v.scalar_tensor_tensor(bonus[:, s, :], r_sb[:, s, :], vecs["u"][:, s:s + 1], k_sb[:, s, :], ALU.mult, ALU.mult)\
                        .then_inc(bonus_ready, 1)

            def wkv_kv(b, c):
                g = c % G
                if c == 0:
                    dve.wait_ge(k_ready, b + 1)
                    dve.wait_ge(vrep_landed, (b + 1) * 16 * G * G)
                    if later(b):
                        dve.wait_ge(reduced, b * SL)
                elif c == AHEAD:
                    dve.wait_ge(front_filled, filled(b, "r"))
                elif c >= NS:
                    dve.wait_ge(reduced, b * SL + (c - NS) // G + 1)
                k_row = k_sb[:, c // G, :].unsqueeze(1).to_broadcast([P, SL, TOK])
                v.tensor_tensor(states[:, buf(c), :, 1:ROW], vrep[:, g, :, :], k_row, ALU.mult).then_inc(kv_ready, 1)

            def wkv_scan(b, c):
                s = c // G
                if c == 0:
                    dve.wait_ge(decay_ready, (b + 1) * SL)
                dve.wait_ge(kv_ready, b * NCH + c + 1)
                dve.wait_ge(row0_ready, b * NCH + c + 1)
                w2 = decay[:, s, :, :].rearrange("p a t -> p (a t)")
                for half in range(2):
                    st = states[:, buf(c), 2 * half:2 * half + 2, :].rearrange("p a t -> p (a t)")
                    v.tensor_tensor_scan(st, w2, st, 0.0, ALU.mult, ALU.add).then_inc(scanned, 1)

            def wkv_prod(b, c):
                dve.wait_ge(scanned, b * 2 * NCH + 2 * c + 2)
                r_row = r_sb[:, c // G, :].unsqueeze(1).to_broadcast([P, SL, TOK])
                st = states[:, buf(c), :, 0:TOK]
                v.tensor_tensor(st, st, r_row, ALU.mult).then_inc(prod_ready, 1)

            def wkv_bonus_v(b):
                dve.wait_ge(back_filled["bonus"], b + 1)
                dve.wait_ge(vrep_landed, (b + 1) * 16 * G * G)
                c_row = back0[:, 0:TOK].unsqueeze(1).to_broadcast([P, SL, TOK])
                v.tensor_tensor(v_sb[:, :, :], v_sb[:, :, :], c_row, ALU.mult).then_inc(bonus_v_ready, 1)

            def wkv_finish(b):
                dve.wait_ge(reduced, (b + 1) * SL)
                dve.wait_ge(bonus_v_ready, b + 1)
                v.tensor_tensor(y[:, :, :], slots(back1), v_sb[:, :, :], ALU.add).then_inc(y_ready, 1)

            def back_centre(b):
                dve.wait_ge(back_filled["mean"], b + 1)
                m_row = back0[:, 0:TOK].unsqueeze(1).to_broadcast([P, SL, TOK])
                v.tensor_tensor(y[:, :, :], y[:, :, :], m_row, ALU.subtract).then_inc(centred, 1)

            def back_scale(b):
                dve.wait_ge(gvar_ready, b + 1)
                v.reciprocal(rstd[:, :], rstd[:, :]).then_inc(grstd_ready, 1)
                dve.wait_ge(sq_ready, b + 1)
                dve.wait_ge(grstd_ready, b + 1)
                r_row = rstd[:, :].unsqueeze(1).to_broadcast([P, SL, TOK])
                v.tensor_tensor(y[:, :, :], y[:, :, :], r_row, ALU.mult).then_inc(normed, 1)

            def back_gate(b):
                dve.wait_ge(affine, (b + 1) * SL)
                v.scalar_tensor_tensor(y[:, :, :], y[:, :, :], 0.5, gate[:, :, :], ALU.mult, ALU.mult).then_inc(gated, 1)

            def back_ln(b):
                dve.wait_ge(back_filled["wo"], b + 1)
                ps = halves(back0)
                dve.wait_ge(res_ready, b + 1)
                v.tensor_tensor(x_res[:, :, :], ps, x_res[:, :, :], ALU.add).then_inc(x1_ready, 1)
                dve.wait_ge(x1_ready, b + 1)
                layer_norm(b, x_res, xn2, stat2_ready, mv2_ready, lvar2_ready, lrstd2_ready, xn2_ready)

            def back_shift(b):
                dve.wait_ge(xc_ready, (b + 1) * (1 + SL))
                v.tensor_tensor(sx2[:, :, :], xc[:, :, 0:TOK], xc[:, :, 1:ROW], ALU.subtract).then_inc(sx2_ready, 1)
                dve.wait_ge(sx2_ready, b + 1)
                for dst, w, s_ready in ((xk2, "ffn_k", xk2_ready), (xr2, "ffn_r", xr2_ready)):
                    for s in range(SL):
                        v.scalar_tensor_tensor(dst[:, s, :], sx2[:, s, :], vecs[w][:, s:s + 1], xc[:, s, 1:ROW], ALU.mult, ALU.add)\
                            .then_inc(s_ready, 1)

            def back_out(b):
                dve.wait_ge(back_filled["fv"], b + 1)
                ps = halves(back0)
                dve.wait_ge(rr_ready, b + 1)
                v.scalar_tensor_tensor(o_sb, o_sb, 1.0, ps, ALU.add, ALU.mult).then_inc(gated_ffn, 1)
                dve.wait_ge(gated_ffn, b + 1)
                v.scalar_tensor_tensor(x_res[:, :, :], o_sb, 0.5, x_res[:, :, :], ALU.mult, ALU.add).then_inc(out_ready, 1)

            def phase_a(b, tail, nb):
                wkv_bonus(b)
                if tail is not None: back_shift(tail)
                wkv_prod(b, 0)
                wkv_bonus_v(b)
                for c in range(1, AHEAD):
                    wkv_prod(b, c)
                wkv_kv(b, AHEAD)
                for c in range(AHEAD, NCH):
                    wkv_scan(b, c)
                    if c + 1 < NCH: wkv_kv(b, c + 1)
                    wkv_prod(b, c)
                    if nb is not None and c == 6: front_scores(nb)
                    if nb is not None and c == 7: front_inverse(nb)
                    if tail is not None and c == 8: back_out(tail)
                    if nb is not None and c == 11: front_ln(nb)
                    if c == 12: front_gate(b)
                    if nb is not None and c == 13: front_shift(nb)
                    if nb is not None and c == 15: mix(nb, MIX_V)
                wkv_finish(b)
                if nb is not None: mix(nb, MIX_W)

            def phase_b(b, nb):
                if b is not None: back_centre(b)
                if nb is not None: mix(nb, MIX_K)
                if nb is not None: mix(nb, MIX_R)
                if b is not None: back_scale(b)
                if b is not None: back_gate(b)
                if nb is not None:
                    mix(nb, MIX_G)
                    for c in range(AHEAD):
                        wkv_kv(nb, c)
                        wkv_scan(nb, c)
                if b is not None: back_ln(b)

            v.memset(eps_col[:, :], EPS).then_inc(consts_set, 1)
            v.memset(half_neg[:, :], -0.5).then_inc(consts_set, 1)
            v.memset(decay[:, :, :, 0:1], 0.0).then_inc(consts_set, 1)
            dve.wait_ge(consts_set, 3)
            dve.wait_ge(w_l0, W_L0)
            front_scores(0)
            front_inverse(0)
            front_ln(0)
            dve.wait_ge(w_mix, W_MIX)
            front_shift(0)
            mix(0, MIX_V)
            mix(0, MIX_W)
            phase_b(None, 0)
            dve.wait_ge(w_back, W_BACK)
            phase_a(0, None, 1)
            phase_b(0, 1)
            with dve.Fori(1, B - 1) as b:
                phase_a(b, b - 1, b + 1)
                phase_b(b, b + 1)
            phase_a(B - 1, B - 2, None)
            phase_b(B - 1, None)
            back_shift(B - 1)
            back_out(B - 1)

        @block.scalar
        def _(act):
            a = nc.scalar.activation

            def front_qk(b):
                act.wait_ge(front_filled, filled(b, "qk"))
                ps = front_unit("qk")
                a(qk[:, 0, :], ps[0:DQ, 0:E], ACT.Identity, bias=bq[:, 0:1]).then_inc(qk_ready, 1)
                a(qk[:, 1, :], ps[0:DQ, E:2 * E], ACT.Identity, bias=bk[:, 0:1]).then_inc(qk_ready, 1)

            def front_v0(b, tail):
                act.wait_ge(front_filled, filled(b, "v0"))
                ps = front_unit("v0")
                if tail is not None:
                    act.wait_ge(xr2_ready, (tail + 1) * SL)
                a(vT[:, :, :].rearrange("p m c -> p (m c)"), ps[:, :], ACT.Copy).then_inc(vT_ready, 1)

            def front_exp(b, tail):
                if tail is not None:
                    act.wait_ge(back_filled["fr"], tail + 1)
                for use, n0 in (("s01", 0), ("s23", 2)):
                    act.wait_ge(front_filled, filled(b, use))
                    ps = halves(front_unit(use))
                    for n in (n0, n0 + 1):
                        act.wait_ge(max_ready, b * NT + n + 1)
                        ins = a(attn[:, n, :], ps[:, n - n0, :], ACT.Exp, bias=score_max[:, n:n + 1], accum_out=row_sum[:, n:n + 1])
                        ins.then_inc(exp_ready, 1)

            def front_normalise(b):
                for n in range(NT):
                    act.wait_ge(inv_ready, b * NT + n + 1)
                    a(attn[:, n, :], attn[:, n, :], ACT.Copy, scale=row_inv[:, n:n + 1]).then_inc(attn_ready, 1)

            def front_attnT(b, tail):
                for use, m0 in (("t01", 0), ("t23", 2)):
                    if tail is not None and m0 == 0:
                        act.wait_ge(back_filled["fv"], tail + 1)
                    elif tail is not None:
                        act.wait_ge(out_ready, tail + 1)
                    act.wait_ge(front_filled, filled(b, use))
                    a(attnT[:, m0:m0 + 2, :], halves(front_unit(use)), ACT.Copy).then_inc(attnT_ready, 1)

            def front_xa(b):
                act.wait_ge(prev_att_landed, (b + 1) * 16 * G)
                if later(b):
                    act.wait_ge(xm_ready, b * NMIX)
                a(xa[:, :, 0], prev_att[:, :], ACT.Copy).then_inc(xa_ready, 1)
                act.wait_ge(front_filled, filled(b, "xnT"))
                ps = slots(front_unit("xnT"))
                for s in range(SL):
                    last = a(xa[:, s, 1:ROW], ps[:, s, :], ACT.Identity, bias=vecs["ln1_b"][:, s:s + 1], scale=vecs["ln1_w"][:, s:s + 1])
                    last.then_inc(xa_ready, 1)

            def front_h(b):
                act.wait_ge(front_filled, filled(b, "w1"))
                ps = front_unit("w1")
                a(h_a[:, :], ps[:, 0:TOK], ACT.Tanh).then_inc(h_ready, 1)
                a(h_b[:, :], ps[DD:DD + DM, E:E + TOK], ACT.Tanh).then_inc(h_ready, 1)

            def td_hidden(b):
                act.wait_ge(front_filled, filled(b, "td1"))
                ps = front_unit("td1")
                a(tw[:, :], ps[0:DD, 0:TOK], ACT.Tanh).then_inc(tw_ready, 1)

            def td_out(b):
                act.wait_ge(front_filled, filled(b, "td2"))
                ps = slots(front_unit("td2"))
                if later(b):
                    act.wait_ge(gated, b)
                for s in range(SL):
                    a(rate[:, s, :], ps[:, s, :], ACT.Exp, bias=vecs["time_decay"][:, s:s + 1]).then_inc(rate_ready, 1)
                act.wait_ge(rate_ready, (b + 1) * SL)
                if later(b):
                    act.wait_ge(scanned, b * 2 * NCH)
                for s in range(SL):
                    a(decay[:, s, :, 1:ROW], rate[:, s, :].unsqueeze(1).to_broadcast([P, 2, TOK]), ACT.Exp, scale=-1.0).then_inc(decay_ready, 1)

            def evacuate(b, use, dst, ready, former, per):
                act.wait_ge(front_filled, filled(b, use))
                ps = front_unit(use)
                if later(b):
                    act.wait_ge(former, b * per)
                a(dst.rearrange("p s t -> p (s t)"), ps[:, :], ACT.Copy).then_inc(ready, 1)

            def front_th(b):
                act.wait_ge(front_filled, filled(b + 1, "g"))
                ps = front_unit("g")
                if later(b):
                    act.wait_ge(gated, b)
                a(gate[:, :, :].rearrange("p s t -> p (s t)"), ps[:, :], ACT.Tanh, scale=0.5).then_inc(th_ready, 1)

            def save_residual(b):
                act.wait_ge(x_mid_ready, (b + 1) * CT)
                if later(b):
                    act.wait_ge(out_stored, b * 16)
                a(x_res[:, :, :], x_mid[:, :, :], ACT.Copy).then_inc(res_ready, 1)

            def wkv_row0(b, c):
                s, g = divmod(c, G)
                if c == 0:
                    act.wait_ge(state_landed, (b + 1) * 16 * G)
                    if later(b):
                        act.wait_ge(reduced, b * SL)
                elif c == AHEAD:
                    act.wait_ge(front_filled, filled(b, "r"))
                if c >= NS:
                    act.wait_ge(reduced, b * SL + (c - NS) // G + 1)
                a(states[:, buf(c), :, 0], state0[:, s * D + g * SL:s * D + (g + 1) * SL], ACT.Copy).then_inc(row0_ready, 1)

            def back_square(b):
                act.wait_ge(centred, b + 1)
                a(sq[:, :, :], y[:, :, :], ACT.Square).then_inc(sq_ready, 1)

            def back_gvar(b):
                act.wait_ge(back_filled["var"], b + 1)
                ps = back1
                a(rstd[:, :], ps[:, 0:TOK], ACT.Sqrt, bias=eps_col[:, 0:1]).then_inc(gvar_ready, 1)

            def back_affine(b):
                act.wait_ge(normed, b + 1)
                for s in range(SL):
                    a(y[:, s, :], y[:, s, :], ACT.Identity, bias=vecs["gn_b"][:, s:s + 1], scale=vecs["gn_w"][:, s:s + 1]).then_inc(affine, 1)

            def back_xc(b):
                act.wait_ge(prev_ffn_landed, (b + 1) * 16 * G)
                a(xc[:, :, 0], prev_ffn[:, :], ACT.Copy).then_inc(xc_ready, 1)
                act.wait_ge(back_filled["xcT"], b + 1)
                ps = slots(back1)
                for s in range(SL):
                    a(xc[:, s, 1:ROW], ps[:, s, :], ACT.Identity, bias=vecs["ln2_b"][:, s:s + 1], scale=vecs["ln2_w"][:, s:s + 1]).then_inc(xc_ready, 1)

            def back_kk(b):
                act.wait_ge(back_filled["fk"], b + 1)
                ps = slots(back0)
                a(kk, ps, ACT.Relu).then_inc(relu_ready, 1)
                act.wait_ge(relu_ready, b + 1)
                a(kk, kk, ACT.Square).then_inc(kk_ready, 1)

            def back_rr(b):
                act.wait_ge(back_filled["fr"], b + 1)
                ps = halves(back0)
                a(o_sb, ps, ACT.Tanh, scale=0.5).then_inc(rr_ready, 1)

            def phase_a(b, tail, nb):
                if tail is not None: back_xc(tail)
                for c in range(AHEAD, NS):
                    wkv_row0(b, c)
                if nb is not None: front_qk(nb)
                if nb is not None: front_v0(nb, tail)
                if tail is not None: back_kk(tail)
                if tail is not None: back_rr(tail)
                for c in range(NS, G + NS):
                    wkv_row0(b, c)
                if nb is not None:
                    front_exp(nb, tail)
                    front_normalise(nb)
                    front_attnT(nb, tail)
                save_residual(b)
                for c in range(G + NS, NCH):
                    wkv_row0(b, c)
                front_th(b)
                if nb is not None:
                    front_xa(nb)
                    front_h(nb)

            def phase_b(b, nb):
                if nb is not None: evacuate(nb, "v", v_sb[:, :, :], v_ready, y_ready, 1)
                if b is not None: back_square(b)
                if nb is not None: td_hidden(nb)
                if b is not None: back_gvar(b)
                if b is not None: back_affine(b)
                if nb is not None:
                    evacuate(nb, "k", k_sb[:, :, :], k_ready, kv_ready, NCH)
                    td_out(nb)
                    for c in range(AHEAD):
                        wkv_row0(nb, c)
                    evacuate(nb, "r", r_sb[:, :, :], r_ready, prod_ready, NCH)

            act.wait_ge(consts_set, 3)
            act.wait_ge(w_l0, W_L0)
            front_qk(0)
            front_v0(0, None)
            front_exp(0, None)
            front_normalise(0)
            front_attnT(0, None)
            act.wait_ge(w_mix, W_MIX)
            front_xa(0)
            front_h(0)
            phase_b(None, 0)
            act.wait_ge(w_back, W_BACK)
            phase_a(0, None, 1)
            phase_b(0, 1)
            with act.Fori(1, B - 1) as b:
                phase_a(b, b - 1, b + 1)
                phase_b(b, b + 1)
            phase_a(B - 1, B - 2, None)
            phase_b(B - 1, None)
            back_xc(B - 1)
            back_kk(B - 1)
            back_rr(B - 1)

        @block.gpsimd
        def _(pool):
            g_ = nc.gpsimd

            def ln_power(b, lvar_s, lrstd_s):
                pool.wait_ge(lvar_s, b + 1)
                g_.tensor_tensor(ln_rstd[:, :], ln_var[:, :], half_neg[:, 0:1].to_broadcast([P, CT]), ALU.pow).then_inc(lrstd_s, 1)

            def mix_add(b, n):
                pool.wait_ge(mixed, b * NMIX + n + 1)
                g_.tensor_tensor(xm[n], xm[n], xa[:, :, 1:ROW], ALU.add).then_inc(xm_ready, 1)

            def store(b):
                pool.wait_ge(out_ready, b + 1)
                pool.dma_start(out_dram[b, :, :].rearrange("(c p) n -> p c n", p=P), x_res[:, :, :]).then_inc(out_stored, 16)

            def phase_a(b, tail, nb):
                if tail is not None: store(tail)
                if nb is not None:
                    ln_power(nb, lvar_ready, lrstd_ready)
                    mix_add(nb, 0)
                    mix_add(nb, 1)

            def phase_b(b, nb):
                if nb is not None:
                    mix_add(nb, 2)
                    mix_add(nb, 3)
                    mix_add(nb, 4)
                if b is not None: ln_power(b, lvar2_ready, lrstd2_ready)

            pool.wait_ge(consts_set, 3)
            ln_power(0, lvar_ready, lrstd_ready)
            mix_add(0, 0)
            mix_add(0, 1)
            phase_b(None, 0)
            phase_a(0, None, 1)
            phase_b(0, 1)
            with pool.Fori(1, B - 1) as b:
                phase_a(b, b - 1, b + 1)
                phase_b(b, b + 1)
            phase_a(B - 1, B - 2, None)
            phase_b(B - 1, None)
            store(B - 1)


def kernel(**inputs):
    import numpy as np
    import concourse.bacc as bacc
    from concourse import mybir as _mybir
    from concourse.bass_utils import run_bass_kernel_spmd as run

    def t(name):
        return np.asarray(inputs[name])

    def channels(w, axis):
        shape = w.shape
        w = w.reshape(shape[:axis] + (H, G, SL) + shape[axis + 1:]).swapaxes(axis, axis + 1)
        return w.reshape(shape[:axis] + (P, SL) + shape[axis + 1:])

    def proj(name):
        return channels(channels(t(name).T, 1), 0).swapaxes(2, 3)

    pre0, pre1 = "L0_xattn_", "L1_xattn_"
    part = np.arange(P)
    same_head = (part[:, None] % H == part[None, :] % H).astype(np.float32)
    arrays = {
        "x": t("x"), "ctx": t("ctx_2048"),
        "wq": t(pre0 + "Wq").T.reshape(CT, P, DQ).transpose(1, 0, 2),
        "wk": t(pre0 + "Wk").T.reshape(CT, P, DQ).transpose(1, 0, 2),
        "wv": t(pre0 + "Wv").T.reshape(CT, P, TOK).transpose(1, 0, 2),
        "bq": t(pre0 + "bq").reshape(DQ, 1), "bk": t(pre0 + "bk").reshape(DQ, 1),
        "bv": t(pre0 + "bv").reshape(CT, P).T,
        "ident": np.eye(P, dtype=np.float32), "red": same_head[:, 0:H],
        "head_sum": same_head, "head_mean": same_head * np.float32(1.0 / D),
        "maa_stack": channels(t(pre1 + "maa_stack").reshape(NMIX, E), 1).transpose(1, 0, 2),
        "maa_w1": channels(t(pre1 + "maa_w1"), 0),
        "maa_w2": channels(t(pre1 + "maa_w2").reshape(NMIX * DM, E), 1).transpose(0, 2, 1),
        "td_w1": channels(t(pre1 + "td_w1"), 0),
        "td_w2": channels(t(pre1 + "td_w2"), 1).transpose(0, 2, 1),
        "ffn_k": channels(t(pre1 + "ffn_maa_k"), 0), "ffn_r": channels(t(pre1 + "ffn_maa_r"), 0),
        "Wo": channels(t(pre1 + "Wo").T, 0), "Wfr": channels(t(pre1 + "Wfr").T, 0), "Wfv": channels(t(pre1 + "Wfv").T, 0),
    }
    for n in ["ln1_w", "ln1_b", "maa_x", "time_decay", "u", "gn_w", "gn_b", "ln2_w", "ln2_b"]:
        arrays[n] = channels(t(pre1 + n).reshape(E), 0)
    for n in ["Wr", "Wk", "Wv", "Wg", "Wfk"]:
        arrays[n] = proj(pre1 + n)

    nc = bacc.Bacc("TRN2", target_bir_lowering=False, num_devices=1)
    io, given = {}, {}
    for n in _INS:
        arr = np.ascontiguousarray(arrays[n])
        given[f"in_{n}"] = arr
        io[n] = nc.dram_tensor(f"in_{n}", arr.shape, _mybir.dt.from_np(arr.dtype), kind="ExternalInput").ap()
    out = nc.dram_tensor("out", (B, TOK, E), _mybir.dt.float32, kind="ExternalOutput").ap()
    xattn_rwkv_kernel(nc, io, out)
    result = run(nc, [given], core_ids=[0])
    return result.results[0]["out"]
```

```python
from contextlib import ExitStack

import concourse.bass as bass
from concourse import mybir

ALU = mybir.AluOpType
ACT = mybir.ActivationFunctionType
AX_X = mybir.AxisListType.X
F32 = mybir.dt.float32

P = 128
B, TOK, E = 8, 256, 512
CT = TOK // P
NT = E // P
DQ = 32
H, D = 32, 16
SL = E // P
G = D // SL
DM, DD = 32, 64
NMIX = 5
MIX_K, MIX_W, MIX_V, MIX_R, MIX_G = range(NMIX)
MIX_ORDER = [MIX_V, MIX_W, MIX_K, MIX_R, MIX_G]
ROW = TOK + 1
NCH = G * SL
AHEAD = 3
BEHIND = 3
NS = 7
EPS = 1e-5

FRONT_USES = ["qk", "v0", "s01", "s23", "t01", "t23", "out", "xnT", "w1",
              "m2", "m1", "v", "m0", "k", "td2", "m3", "r", "m4"]
NF = len(FRONT_USES)
USE = {n: i for i, n in enumerate(FRONT_USES)}

_INS = ["x", "ctx", "wq", "wk", "wv", "bq", "bk", "bv", "ident", "red", "head_sum", "head_mean",
        "ln1_w", "ln1_b", "maa_x", "maa_stack", "maa_w1", "maa_w2", "td_w1", "td_w2", "time_decay", "u",
        "Wr", "Wk", "Wv", "Wg", "Wo", "gn_w", "gn_b", "ln2_w", "ln2_b", "ffn_k", "ffn_r", "Wfk", "Wfr", "Wfv"]


def xattn_rwkv_kernel(nc, io, out_dram):
    with ExitStack() as ctx:
        def sb(name, *shape):
            return ctx.enter_context(nc.sbuf_tensor(name, list(shape), F32))

        def psum(name, *shape):
            return ctx.enter_context(nc.psum_tensor(name, list(shape), F32))

        def sem(name):
            return ctx.enter_context(nc.semaphore(name))

        wq, wk = sb("wq", P, CT, DQ), sb("wk", P, CT, DQ)
        wv = sb("wv", P, CT, TOK)
        bq, bk, bv = sb("bq", DQ, 1), sb("bk", DQ, 1), sb("bv", P, CT)
        ident = sb("ident", P, P)
        red = sb("red", P, H)
        head_sum, head_mean = sb("head_sum", P, P), sb("head_mean", P, P)
        vecs = {n: sb(n, P, SL) for n in ["ln1_w", "ln1_b", "maa_x", "time_decay", "u", "gn_w", "gn_b",
                                          "ln2_w", "ln2_b", "ffn_k", "ffn_r"]}
        maa_stack = sb("maa_stack", P, NMIX, SL)
        maa_w1 = sb("maa_w1", P, SL, NMIX * DM)
        maa_w2a = sb("maa_w2a", P, SL, P)
        low_rank = sb("low_rank", DD + DM, SL, P)
        td_w2, maa_w2b = low_rank[0:DD], low_rank[DD:DD + DM]
        td_w1 = sb("td_w1", P, SL, DD)
        w_proj = {n: sb(n, P, SL, SL, P) for n in ["Wr", "Wk", "Wv", "Wg", "Wfk"]}
        w_tok = {n: sb(n, P, SL, E) for n in ["Wo", "Wfr", "Wfv"]}
        wait_col = sb("wait_col", P, 1)
        eps_col = sb("eps_col", P, 1)
        half_neg = sb("half_neg", P, 1)

        x_in, ctx_in = sb("x_in", P, CT, E), sb("ctx_in", P, CT, E)
        prev_att, prev_ffn = sb("prev_att", P, SL), sb("prev_ffn", P, SL)
        state0 = sb("state0", P, SL * D)
        reg_a = sb("reg_a", P, NT, E)
        reg_b = sb("reg_b", P, NT, E)
        reg_c = sb("reg_c", P, NT, TOK)
        reg_d = sb("reg_d", P, 2, E)
        x_mid, x_res = sb("x_mid", P, CT, E), sb("x_res", P, CT, E)
        xa, xc = sb("xa", P, SL, ROW), sb("xc", P, SL, ROW)
        sx = sb("sx", P, SL, TOK)
        h_a = sb("h_a", P, TOK)
        low_act = sb("low_act", DD + DM, TOK)
        tw, h_b = low_act[0:DD], low_act[DD:DD + DM]
        decay = sb("decay", P, SL, 2, ROW)
        vrep = sb("vrep", P, G, SL, TOK)
        k_sb, v_sb, r_sb, gate = (sb(n, P, SL, TOK) for n in ["k_sb", "v_sb", "r_sb", "gate"])
        states = sb("states", P, NS, SL, ROW)
        y = sb("y", P, SL, TOK)
        rstd = sb("rstd", P, TOK)
        score_max, row_sum, row_inv = sb("score_max", P, NT), sb("row_sum", P, NT), sb("row_inv", P, NT)
        ln_stat, ln_mv, ln_var, ln_rstd = sb("ln_stat", P, CT, 6), sb("ln_mv", P, CT, 2), sb("ln_var", P, CT), sb("ln_rstd", P, CT)

        attn, attnT = reg_a, reg_b
        xn = reg_a[:, 0:2, :]
        xpre = reg_a[:, 2:4, :].rearrange("p a (c t) -> p (a c) t", t=TOK)
        xk2 = reg_a[:, 0:2, :].rearrange("p a (c t) -> p (a c) t", t=TOK)
        xr2 = xpre
        kk = reg_b[:, 0:2, :].rearrange("p a (c t) -> p (a c) t", t=TOK)
        o_sb = reg_b[:, 2:4, :]
        vT = reg_c
        xn2 = reg_c[:, :, :].rearrange("p (c a) t -> p c (a t)", c=CT)
        sx2 = reg_c
        qk = reg_d[0:DQ, :, :]
        sq = reg_d[:, :, :].rearrange("p a (c t) -> p (a c) t", t=TOK)
        bonus = kk
        bonus_v = y
        rate = states[:, 5, :, 0:TOK]
        xm = [states[:, n, :, 0:TOK] for n in (2, 3, 1, 4)] + [sx[:, :, :]]

        front = [psum("front0", P, 1024), psum("front1", P, 1024)]
        back = [psum("back0", P, 1024), psum("back1", P, 1024)]

        def slots(ps):
            return ps[:, :].rearrange("p (s t) -> p s t", t=TOK)

        def halves(ps):
            return ps[:, :].rearrange("p (c n) -> p c n", c=2)

        w_qk, w_l0, w_mix, w_wkv, w_back = sem("w_qk"), sem("w_l0"), sem("w_mix"), sem("w_wkv"), sem("w_back")
        x_landed, ctx_landed, prev_att_landed = sem("x_landed"), sem("ctx_landed"), sem("prev_att_landed")
        prev_ffn_landed, state_landed, out_stored = sem("prev_ffn_landed"), sem("state_landed"), sem("out_stored")
        consts_set = sem("consts_set")
        front_filled = sem("front_filled")
        back_filled = {u: sem(f"{u}_filled") for u in ["bonus", "xcT", "fk", "fr", "fv", "g", "td1", "mean", "wo", "var"]}
        qk_ready = sem("qk_ready")
        vT_ready = sem("vT_ready")
        max_ready = sem("max_ready")
        exp_ready = sem("exp_ready")
        inv_ready = sem("inv_ready")
        attn_ready = sem("attn_ready")
        attnT_ready = sem("attnT_ready")
        x_mid_ready = sem("x_mid_ready")
        stat_ready = sem("stat_ready")
        mv_ready = sem("mv_ready")
        lvar_ready = sem("lvar_ready")
        lrstd_ready = sem("lrstd_ready")
        xn_ready = sem("xn_ready")
        xa_ready = sem("xa_ready")
        sx_ready = sem("sx_ready")
        xpre_ready = sem("xpre_ready")
        h_ready = sem("h_ready")
        mixed = sem("mixed")
        xm_ready = sem("xm_ready")
        tw_ready = sem("tw_ready")
        rate_ready = sem("rate_ready")
        decay_ready = sem("decay_ready")
        k_ready, v_ready, r_ready = sem("k_ready"), sem("v_ready"), sem("r_ready")
        vrep_landed = sem("vrep_landed")
        th_ready, gate_ready = sem("th_ready"), sem("gate_ready")
        res_ready = sem("res_ready")
        bonus_ready = sem("bonus_ready")
        kv_ready, row0_ready, scanned = sem("kv_ready"), sem("row0_ready"), sem("scanned")
        prod_ready, reduced = sem("prod_ready"), sem("reduced")
        bonus_v_ready, y_ready = sem("bonus_v_ready"), sem("y_ready")
        centred, sq_ready, gvar_ready, grstd_ready = sem("centred"), sem("sq_ready"), sem("gvar_ready"), sem("grstd_ready")
        normed, affine, gated = sem("normed"), sem("affine"), sem("gated")
        x1_ready = sem("x1_ready")
        stat2_ready, mv2_ready, lvar2_ready, lrstd2_ready = sem("stat2_ready"), sem("mv2_ready"), sem("lvar2_ready"), sem("lrstd2_ready")
        xn2_ready = sem("xn2_ready")
        xc_ready = sem("xc_ready")
        sx2_ready, xk2_ready, xr2_ready = sem("sx2_ready"), sem("xk2_ready"), sem("xr2_ready")
        relu_ready, kk_ready = sem("relu_ready"), sem("kk_ready")
        rr_ready, gated_ffn, out_ready = sem("rr_ready"), sem("gated_ffn"), sem("out_ready")

        block = ctx.enter_context(nc.Block())

        def later(b):
            return not (isinstance(b, int) and b == 0)

        def buf(c):
            return (c + NS - 1) % NS

        def filled(b, use):
            return b * NF + USE[use] + 1

        def front_unit(use):
            return front[USE[use] % 2]

        FRONT_DRAINED = {
            "qk": (qk_ready, 2, 2), "v0": (vT_ready, 1, 1), "s01": (exp_ready, NT, 2), "s23": (exp_ready, NT, NT),
            "t01": (attnT_ready, 2, 1), "t23": (attnT_ready, 2, 2), "out": (x_mid_ready, CT, CT), "xnT": (xa_ready, 1 + SL, 1 + SL),
            "w1": (h_ready, 2, 2), "td2": (rate_ready, SL, SL),
            "k": (k_ready, 1, 1), "v": (v_ready, 1, 1), "r": (r_ready, 1, 1)}
        FRONT_DRAINED.update({f"m{f}": (mixed, NMIX, n + 1) for n, f in enumerate(MIX_ORDER)})

        def has_former(b, use):
            return later(b) or USE[use] >= 2

        def former_drained(b, use):
            before = USE[use] - 2
            s, per, n = FRONT_DRAINED[FRONT_USES[before % NF]]
            return (s, b * per + n) if before >= 0 else (s, b * per)

        back0, back1 = back

        @block.sync
        def _(sp):
            def load(dst, name, s):
                sp.dma_start(dst, io[name]).then_inc(s, 16)

            def by_group(row, n):
                return row.rearrange("(h g n) -> g h n", g=G, n=n)

            def load_inputs(b):
                if later(b):
                    sp.wait_ge(x_mid_ready, b * CT)
                sp.dma_start(x_in[:, :, :], io["x"][b, :, :].rearrange("(c p) n -> p c n", p=P)).then_inc(x_landed, 16)
                sp.dma_start(ctx_in[:, :, :], io["ctx"][b, :, :].rearrange("(c p) n -> p c n", p=P)).then_inc(ctx_landed, 16)
                if later(b):
                    sp.wait_ge(xa_ready, b * (1 + SL))
                for g in range(G):
                    sp.dma_start(prev_att[H * g:H * (g + 1), :], by_group(io["ctx"][b, 1, :], SL)[g]).then_inc(prev_att_landed, 16)

            def load_state(b):
                if later(b):
                    sp.wait_ge(row0_ready, b * NCH)
                for g in range(G):
                    sp.dma_start(state0[H * g:H * (g + 1), :], by_group(io["ctx"][b, 2:2 + D, :].rearrange("r e -> (r e)"), SL * D)[g])\
                        .then_inc(state_landed, 16)

            def load_prev_ffn(b):
                if later(b):
                    sp.wait_ge(xc_ready, b * (1 + SL))
                for g in range(G):
                    sp.dma_start(prev_ffn[H * g:H * (g + 1), :], by_group(io["ctx"][b, 0, :], SL)[g]).then_inc(prev_ffn_landed, 16)

            def store(b):
                sp.wait_ge(out_ready, b + 1)
                sp.dma_start(out_dram[b, :, :].rearrange("(c p) n -> p c n", p=P), x_res[:, :, :]).then_inc(out_stored, 16)

            def replicate(b):
                sp.wait_ge(v_ready, b + 1)
                if later(b):
                    sp.wait_ge(kv_ready, b * NCH)
                for g in range(G):
                    for to in range(G):
                        sp.dma_start(vrep[H * to:H * (to + 1), g, :, :], v_sb[H * g:H * (g + 1), :, :]).then_inc(vrep_landed, 16)

            for name, dst in [("wq", wq), ("bq", bq), ("wk", wk), ("bk", bk)]:
                load(dst[:], name, w_qk)
            load_inputs(0)
            for name, dst in [("wv", wv), ("bv", bv), ("ident", ident)]:
                load(dst[:], name, w_l0)
            load_state(0)
            load_prev_ffn(0)
            for name in ["ln1_w", "ln1_b", "maa_x", "time_decay", "u"]:
                load(vecs[name][:], name, w_mix)
            load(maa_stack[:], "maa_stack", w_mix)
            load(maa_w1[:], "maa_w1", w_mix)
            sp.dma_start(maa_w2a[:], io["maa_w2"][0:P, :, :]).then_inc(w_mix, 16)
            sp.dma_start(maa_w2b[:], io["maa_w2"][P:P + DM, :, :]).then_inc(w_mix, 16)
            load(td_w1[:], "td_w1", w_mix)
            load(td_w2[:], "td_w2", w_mix)
            for name in ["Wk", "Wv", "Wr", "Wg"]:
                load(w_proj[name][:], name, w_wkv)
            for name, dst in [("red", red), ("head_sum", head_sum)]:
                load(dst[:], name, w_wkv)
            load(head_mean[:], "head_mean", w_back)
            for name in ["gn_w", "gn_b", "ln2_w", "ln2_b", "ffn_k", "ffn_r"]:
                load(vecs[name][:], name, w_back)
            for name in ["Wo", "Wfr", "Wfv"]:
                load(w_tok[name][:], name, w_back)
            load(w_proj["Wfk"][:], "Wfk", w_back)
            replicate(0)
            load_inputs(1)
            load_state(1)
            with sp.Fori(2, B) as b:
                replicate(b - 1)
                load_inputs(b)
                load_prev_ffn(b - 1)
                store(b - 2)
                load_state(b)
            replicate(B - 1)
            load_prev_ffn(B - 1)
            store(B - 2)
            store(B - 1)
            sp.wait_ge(out_stored, 16 * B)

        W_QK, W_L0, W_MIX, W_WKV, W_BACK = 16 * 4, 16 * 3, 16 * 11, 16 * 6, 16 * 11

        @block.tensor
        def _(pe):
            mm = nc.tensor.matmul

            def front_qk(b):
                pe.wait_ge(x_landed, (b + 1) * 16)
                pe.wait_ge(ctx_landed, (b + 1) * 16)
                if has_former(b, "qk"):
                    pe.wait_ge(*former_drained(b, "qk"))
                ps = front_unit("qk")
                for c in range(CT):
                    for half, w, src in ((0, wq, x_in), (1, wk, ctx_in)):
                        last = mm(ps[half * DQ:(half + 1) * DQ, half * E:(half + 1) * E], w[:, c, :], src[:, c, :], start=(c == 0), stop=(c == CT - 1))
                last.then_inc(front_filled, 1)

            def front_v0(b):
                pe.wait_ge(ctx_landed, (b + 1) * 16)
                if has_former(b, "v0"):
                    pe.wait_ge(*former_drained(b, "v0"))
                ps = slots(front_unit("v0"))
                for m in range(NT):
                    for c in range(CT):
                        last = mm(ps[:, m, :], ctx_in[:, c, m * P:(m + 1) * P], wv[:, c, :], start=(c == 0), stop=(c == CT - 1))
                last.then_inc(front_filled, 1)

            def front_scores(b):
                pe.wait_ge(qk_ready, (b + 1) * 2)
                for use, n0 in (("s01", 0), ("s23", 2)):
                    if has_former(b, use):
                        pe.wait_ge(*former_drained(b, use))
                    ps = halves(front_unit(use))
                    for n in (n0, n0 + 1):
                        last = mm(ps[:, n - n0, :], qk[:, 0, n * P:(n + 1) * P], qk[:, 1, :], start=True, stop=True)
                    last.then_inc(front_filled, 1)

            def front_transposes(b):
                pe.wait_ge(attn_ready, (b + 1) * NT)
                for use, m0 in (("t01", 0), ("t23", 2)):
                    if has_former(b, use):
                        pe.wait_ge(*former_drained(b, use))
                    ps = halves(front_unit(use))
                    for m in (m0, m0 + 1):
                        for n in range(NT):
                            last = nc.tensor.transpose(ps[:, m - m0, n * P:(n + 1) * P], attn[:, n, m * P:(m + 1) * P], ident[:, :])
                    last.then_inc(front_filled, 1)

            def front_out(b):
                pe.wait_ge(vT_ready, b + 1)
                pe.wait_ge(attnT_ready, (b + 1) * 2)
                if has_former(b, "out"):
                    pe.wait_ge(*former_drained(b, "out"))
                ps = halves(front_unit("out"))
                for c in range(CT):
                    for m in range(NT):
                        last = mm(ps[:, c, :], vT[:, m, c * P:(c + 1) * P], attnT[:, m, :], start=(m == 0), stop=(m == NT - 1))
                last.then_inc(front_filled, 1)

            def front_xnT(b):
                pe.wait_ge(xn_ready, (b + 1) * CT)
                if has_former(b, "xnT"):
                    pe.wait_ge(*former_drained(b, "xnT"))
                ps = slots(front_unit("xnT"))
                for s in range(SL):
                    for c in range(CT):
                        last = nc.tensor.transpose(ps[:, s, c * P:(c + 1) * P], xn[:, c, s * P:(s + 1) * P], ident[:, :])
                last.then_inc(front_filled, 1)

            def front_w1(b):
                pe.wait_ge(xpre_ready, (b + 1) * SL)
                if has_former(b, "w1"):
                    pe.wait_ge(*former_drained(b, "w1"))
                ps = front_unit("w1")
                for lo, hi, p0, off in ((0, P, 0, 0), (P, NMIX * DM, DD, E)):
                    for s in range(SL):
                        last = mm(ps[p0:p0 + hi - lo, off:off + TOK], maa_w1[:, s, lo:hi], xpre[:, s, :], start=(s == 0), stop=(s == SL - 1))
                last.then_inc(front_filled, 1)

            def mix(b, f):
                if f == MIX_ORDER[0]:
                    pe.wait_ge(h_ready, (b + 1) * 2)
                if has_former(b, f"m{f}"):
                    pe.wait_ge(*former_drained(b, f"m{f}"))
                ps = slots(front_unit(f"m{f}"))
                lo = f * DM % P
                w2, h = (maa_w2a, h_a) if f * DM < P else (maa_w2b, h_b)
                for s in range(SL):
                    last = mm(ps[:, s, :], w2[lo:lo + DM, s, :], h[lo:lo + DM, :], start=True, stop=True)
                last.then_inc(front_filled, 1)

            def project(b, use, w, f, mean_of=None):
                n = MIX_ORDER.index(f)
                pe.wait_ge(xm_ready, b * NMIX + n + 1)
                pe.wait_ge(*former_drained(b, use))
                ps = slots(front_unit(use))
                for o in range(SL):
                    for s in range(SL):
                        last = mm(ps[:, o, :], w[:, s, o, :], xm[n][:, s, :], start=(s == 0), stop=(s == SL - 1))
                    if o == SL // 2 - 1 and mean_of is not None:
                        back_mean(mean_of, True)
                last.then_inc(front_filled, 1)

            def project_gate(b, tail, xnT_of):
                pe.wait_ge(xm_ready, (b + 1) * NMIX)
                if tail is not None:
                    pe.wait_ge(gated_ffn, tail + 1)
                else:
                    pe.wait_ge(bonus_v_ready, b + 1)
                for o in range(SL):
                    if o == SL - 1 and xnT_of is not None:
                        front_xnT(xnT_of)
                    for s in range(SL):
                        last = mm(slots(back0)[:, o, :], w_proj["Wg"][:, s, o, :], xm[4][:, s, :], start=(s == 0), stop=(s == SL - 1))
                last.then_inc(back_filled["g"], 1)

            def td_hidden(b):
                pe.wait_ge(xm_ready, b * NMIX + 2)
                if later(b):
                    pe.wait_ge(gate_ready, b)
                ps = back0
                for s in range(SL):
                    last = mm(ps[0:DD, 0:TOK], td_w1[:, s, :], xm[1][:, s, :], start=(s == 0), stop=(s == SL - 1))
                last.then_inc(back_filled["td1"], 1)

            def td_out(b):
                pe.wait_ge(tw_ready, b + 1)
                if has_former(b, "td2"):
                    pe.wait_ge(*former_drained(b, "td2"))
                ps = slots(front_unit("td2"))
                for s in range(SL):
                    last = mm(ps[:, s, :], td_w2[:, s, :], tw[:, :], start=True, stop=True)
                last.then_inc(front_filled, 1)

            def wkv_bonus(b):
                pe.wait_ge(bonus_ready, (b + 1) * SL)
                if later(b):
                    pe.wait_ge(x1_ready, b)
                for s in range(SL):
                    last = mm(back0[:, 0:TOK], head_sum[:, :], bonus[:, s, :], start=(s == 0), stop=(s == SL - 1))
                last.then_inc(back_filled["bonus"], 1)

            def wkv_reduce(b, s):
                pe.wait_ge(prod_ready, b * NCH + G * (s + 1))
                if s == 0 and later(b):
                    pe.wait_ge(xc_ready, b * (1 + SL))
                for half in range(2):
                    for g in range(G):
                        chunk = states[:, buf(s * G + g), 2 * half:2 * half + 2, 0:TOK]
                        last = mm(back1[H * g:H * (g + 1), half * 2 * TOK:(half + 1) * 2 * TOK], red[:, :], chunk,
                                  start=(s == 0), stop=(s == SL - 1))
                last.then_inc(reduced, 1)

            def tok_product(ps, x, w):
                for c in range(CT):
                    for s in range(SL):
                        last = mm(halves(ps)[:, c, :], x[:, s, c * P:(c + 1) * P], w[:, s, :], start=(s == 0), stop=(s == SL - 1))
                return last

            def back_mean(b, b_next):
                pe.wait_ge(y_ready, b + 1)
                if b_next:
                    pe.wait_ge(tw_ready, b + 2)
                for s in range(SL):
                    last = mm(back0[:, 0:TOK], head_mean[:, :], y[:, s, :], start=(s == 0), stop=(s == SL - 1))
                last.then_inc(back_filled["mean"], 1)

            def back_var(b):
                pe.wait_ge(sq_ready, b + 1)
                for s in range(SL):
                    last = mm(back1[:, 0:TOK], head_mean[:, :], sq[:, s, :], start=(s == 0), stop=(s == SL - 1))
                last.then_inc(back_filled["var"], 1)

            def back_wo(b):
                pe.wait_ge(gated, b + 1)
                tok_product(back0, y, w_tok["Wo"]).then_inc(back_filled["wo"], 1)

            def back_xcT(b):
                pe.wait_ge(xn2_ready, (b + 1) * CT)
                for s in range(SL):
                    for c in range(CT):
                        last = nc.tensor.transpose(slots(back1)[:, s, c * P:(c + 1) * P], xn2[:, c, s * P:(s + 1) * P], ident[:, :])
                last.then_inc(back_filled["xcT"], 1)

            def back_fk(b, last_one=False):
                pe.wait_ge(xk2_ready, (b + 1) * SL)
                if not last_one:
                    pe.wait_ge(bonus_v_ready, b + 2)
                for o in range(SL):
                    for s in range(SL):
                        last = mm(slots(back0)[:, o, :], w_proj["Wfk"][:, s, o, :], xk2[:, s, :], start=(s == 0), stop=(s == SL - 1))
                last.then_inc(back_filled["fk"], 1)

            def back_fr(b):
                pe.wait_ge(xr2_ready, (b + 1) * SL)
                pe.wait_ge(relu_ready, b + 1)
                tok_product(back0, xr2, w_tok["Wfr"]).then_inc(back_filled["fr"], 1)

            def back_fv(b):
                pe.wait_ge(kk_ready, b + 1)
                pe.wait_ge(rr_ready, b + 1)
                tok_product(back0, kk, w_tok["Wfv"]).then_inc(back_filled["fv"], 1)

            def phase_a(b, tail, nb):
                if nb is not None: front_qk(nb)
                wkv_bonus(b)
                if tail is not None: back_xcT(tail)
                if nb is not None: front_v0(nb)
                if tail is not None: back_fk(tail)
                wkv_reduce(b, 0)
                if tail is not None: back_fr(tail)
                if nb is not None: front_scores(nb)
                if tail is not None: back_fv(tail)
                if nb is not None: front_transposes(nb)
                wkv_reduce(b, 1)
                if nb is not None: front_out(nb)
                project_gate(b, tail, nb)
                wkv_reduce(b, 2)
                if nb is not None:
                    front_w1(nb)
                    mix(nb, MIX_V)
                    mix(nb, MIX_W)

            def phase_b(b, nb):
                if nb is not None:
                    project(nb, "v", w_proj["Wv"], MIX_V)
                    mix(nb, MIX_K)
                    td_hidden(nb)
                if b is not None: wkv_reduce(b, 3)
                if nb is not None:
                    project(nb, "k", w_proj["Wk"], MIX_K, mean_of=b)
                    td_out(nb)
                    mix(nb, MIX_R)
                else:
                    back_mean(b, False)
                if b is not None: back_var(b)
                if nb is not None: project(nb, "r", w_proj["Wr"], MIX_R)
                if b is not None: back_wo(b)
                if nb is not None: mix(nb, MIX_G)

            pe.wait_ge(w_qk, W_QK)
            front_qk(0)
            pe.wait_ge(w_l0, W_L0)
            front_v0(0)
            front_scores(0)
            front_transposes(0)
            front_out(0)
            front_xnT(0)
            pe.wait_ge(w_mix, W_MIX)
            front_w1(0)
            mix(0, MIX_V)
            mix(0, MIX_W)
            pe.wait_ge(w_wkv, W_WKV)
            phase_b(None, 0)
            pe.wait_ge(w_back, W_BACK)
            phase_a(0, None, 1)
            phase_b(0, 1)
            with pe.Fori(1, B - 1) as b:
                phase_a(b, b - 1, b + 1)
                phase_b(b, b + 1)
            phase_a(B - 1, B - 2, None)
            phase_b(B - 1, None)
            back_xcT(B - 1)
            back_fk(B - 1, last_one=True)
            back_fr(B - 1)
            back_fv(B - 1)

        @block.vector
        def _(dve):
            v = nc.vector

            def front_scores(b):
                for use, n0 in (("s01", 0), ("s23", 2)):
                    dve.wait_ge(front_filled, filled(b, use))
                    ps = halves(front_unit(use))
                    for n in (n0, n0 + 1):
                        if later(b):
                            dve.wait_ge(attn_ready, b * NT)
                        v.tensor_reduce(score_max[:, n:n + 1], ps[:, n - n0, :], AX_X, ALU.max, negate=True).then_inc(max_ready, 1)

            def layer_norm(b, x, dst, stat_s, mv_s, lvar_s, lrstd_s, out_s):
                for c in range(CT):
                    v.bn_stats(ln_stat[:, c, :], x[:, c, :]).then_inc(stat_s, 1)
                dve.wait_ge(stat_s, (b + 1) * CT)
                v.memset(wait_col[:, :], 0.0)
                for c in range(CT):
                    v.bn_aggr(ln_mv[:, c, :], ln_stat[:, c, :]).then_inc(mv_s, 1)
                dve.wait_ge(mv_s, (b + 1) * CT)
                v.tensor_scalar(ln_var[:, :], ln_mv[:, :, 1], EPS, None, ALU.add).then_inc(lvar_s, 1)
                dve.wait_ge(lrstd_s, b + 1)
                for c in range(CT):
                    v.tensor_scalar(dst[:, c, :].rearrange("p (s g h) -> p h g s", s=SL, g=G),
                                    x[:, c, :].rearrange("p (h g s) -> p h g s", s=SL, g=G), ln_mv[:, c, 0:1], ln_rstd[:, c:c + 1], ALU.subtract, ALU.mult).then_inc(out_s, 1)

            def front_inverse(b):
                dve.wait_ge(exp_ready, (b + 1) * NT)
                for n in range(NT):
                    v.reciprocal(row_inv[:, n:n + 1], row_sum[:, n:n + 1]).then_inc(inv_ready, 1)

            def front_ln(b):
                dve.wait_ge(front_filled, filled(b, "out"))
                ps = halves(front_unit("out"))
                if later(b):
                    dve.wait_ge(res_ready, b)
                for c in range(CT):
                    ins = v.scalar_tensor_tensor(x_mid[:, c, :], ps[:, c, :], bv[:, c:c + 1], x_in[:, c, :], ALU.add, ALU.add)
                    ins.then_inc(x_mid_ready, 1)
                dve.wait_ge(x_mid_ready, (b + 1) * CT)
                layer_norm(b, x_mid, xn, stat_ready, mv_ready, lvar_ready, lrstd_ready, xn_ready)

            def front_shift(b):
                dve.wait_ge(xa_ready, (b + 1) * (1 + SL))
                if later(b):
                    dve.wait_ge(back_filled["g"], b)
                v.tensor_tensor(sx[:, :, :], xa[:, :, 0:TOK], xa[:, :, 1:ROW], ALU.subtract).then_inc(sx_ready, 1)
                dve.wait_ge(sx_ready, b + 1)
                for s in range(SL):
                    v.scalar_tensor_tensor(xpre[:, s, :], sx[:, s, :], vecs["maa_x"][:, s:s + 1], xa[:, s, 1:ROW], ALU.mult, ALU.add)\
                        .then_inc(xpre_ready, 1)

            def mix(b, f):
                n = MIX_ORDER.index(f)
                dve.wait_ge(front_filled, filled(b, f"m{f}"))
                ps = slots(front_unit(f"m{f}"))
                if later(b) and n < 3:
                    dve.wait_ge(reduced, b * SL - 1)
                elif later(b) and n < 4:
                    dve.wait_ge(reduced, b * SL)
                elif n == 4:
                    dve.wait_ge(mixed, b * NMIX + 4)
                for s in range(SL):
                    last = v.scalar_tensor_tensor(xm[n][:, s, :], ps[:, s, :], maa_stack[:, f, s:s + 1], sx[:, s, :], ALU.add, ALU.mult)
                last.then_inc(mixed, 1)

            def mix_add(b, f):
                n = MIX_ORDER.index(f)
                dve.wait_ge(mixed, b * NMIX + n + 1)
                v.tensor_tensor(xm[n], xm[n], xa[:, :, 1:ROW], ALU.add).then_inc(xm_ready, 1)

            def front_gate(b):
                dve.wait_ge(back_filled["g"], b + 1)
                ps = back0
                dve.wait_ge(th_ready, b + 1)
                g2 = gate[:, :, :].rearrange("p s t -> p (s t)")
                v.scalar_tensor_tensor(g2, g2, 1.0, ps[:, :], ALU.add, ALU.mult).then_inc(gate_ready, 1)

            def wkv_bonus(b):
                dve.wait_ge(k_ready, b + 1)
                dve.wait_ge(r_ready, b + 1)
                if later(b):
                    dve.wait_ge(front_filled, filled(b, "out"))
                for s in range(SL):
                    v.scalar_tensor_tensor(bonus[:, s, :], r_sb[:, s, :], vecs["u"][:, s:s + 1], k_sb[:, s, :], ALU.mult, ALU.mult)\
                        .then_inc(bonus_ready, 1)

            def wkv_kv(b, c):
                g = c % G
                if c == 0:
                    dve.wait_ge(k_ready, b + 1)
                    dve.wait_ge(vrep_landed, (b + 1) * 16 * G * G)
                    if later(b):
                        dve.wait_ge(reduced, b * SL)
                elif c == 2:
                    dve.wait_ge(front_filled, filled(b, "k"))
                    dve.wait_ge(back_filled["td1"], b + 1)
                elif c == 5:
                    dve.wait_ge(front_filled, filled(b, "r"))
                elif c == 6:
                    dve.wait_ge(decay_ready, (b + 1) * SL)
                elif c >= NS:
                    dve.wait_ge(reduced, b * SL + (c - NS) // G + 1)
                k_row = k_sb[:, c // G, :].unsqueeze(1).to_broadcast([P, SL, TOK])
                v.tensor_tensor(states[:, buf(c), :, 1:ROW], vrep[:, g, :, :], k_row, ALU.mult).then_inc(kv_ready, 1)

            def wkv_scan(b, c):
                s = c // G
                if c == 0:
                    dve.wait_ge(decay_ready, (b + 1) * SL)
                dve.wait_ge(kv_ready, b * NCH + c + 1)
                dve.wait_ge(row0_ready, b * NCH + c + 1)
                w2 = decay[:, s, :, :].rearrange("p a t -> p (a t)")
                for half in range(2):
                    st = states[:, buf(c), 2 * half:2 * half + 2, :].rearrange("p a t -> p (a t)")
                    v.tensor_tensor_scan(st, w2, st, 0.0, ALU.mult, ALU.add).then_inc(scanned, 1)

            def wkv_prod(b, c):
                if c == 0:
                    dve.wait_ge(r_ready, b + 1)
                dve.wait_ge(scanned, b * 2 * NCH + 2 * c + 2)
                r_row = r_sb[:, c // G, :].unsqueeze(1).to_broadcast([P, SL, TOK])
                st = states[:, buf(c), :, 0:TOK]
                v.tensor_tensor(st, st, r_row, ALU.mult).then_inc(prod_ready, 1)

            def wkv_bonus_v(b):
                dve.wait_ge(back_filled["bonus"], b + 1)
                if later(b):
                    dve.wait_ge(back_filled["wo"], b)
                c_row = back0[:, 0:TOK].unsqueeze(1).to_broadcast([P, SL, TOK])
                v.tensor_tensor(bonus_v[:, :, :], v_sb[:, :, :], c_row, ALU.mult).then_inc(bonus_v_ready, 1)

            def wkv_finish(b):
                dve.wait_ge(reduced, (b + 1) * SL)
                dve.wait_ge(bonus_v_ready, b + 1)
                v.tensor_tensor(y[:, :, :], slots(back1), bonus_v[:, :, :], ALU.add).then_inc(y_ready, 1)

            def back_centre(b):
                dve.wait_ge(back_filled["mean"], b + 1)
                m_row = back0[:, 0:TOK].unsqueeze(1).to_broadcast([P, SL, TOK])
                v.tensor_tensor(y[:, :, :], y[:, :, :], m_row, ALU.subtract).then_inc(centred, 1)

            def back_scale(b):
                dve.wait_ge(gvar_ready, b + 1)
                v.reciprocal(rstd[:, :], rstd[:, :]).then_inc(grstd_ready, 1)
                dve.wait_ge(sq_ready, b + 1)
                dve.wait_ge(grstd_ready, b + 1)
                r_row = rstd[:, :].unsqueeze(1).to_broadcast([P, SL, TOK])
                v.tensor_tensor(y[:, :, :], y[:, :, :], r_row, ALU.mult).then_inc(normed, 1)

            def back_gate(b):
                dve.wait_ge(affine, (b + 1) * SL)
                v.scalar_tensor_tensor(y[:, :, :], y[:, :, :], 0.5, gate[:, :, :], ALU.mult, ALU.mult).then_inc(gated, 1)

            def back_ln(b):
                dve.wait_ge(back_filled["wo"], b + 1)
                ps = halves(back0)
                dve.wait_ge(res_ready, b + 1)
                v.tensor_tensor(x_res[:, :, :], ps, x_res[:, :, :], ALU.add).then_inc(x1_ready, 1)
                dve.wait_ge(x1_ready, b + 1)
                layer_norm(b, x_res, xn2, stat2_ready, mv2_ready, lvar2_ready, lrstd2_ready, xn2_ready)

            def back_shift(b):
                dve.wait_ge(xc_ready, (b + 1) * (1 + SL))
                v.tensor_tensor(sx2[:, :, :], xc[:, :, 0:TOK], xc[:, :, 1:ROW], ALU.subtract).then_inc(sx2_ready, 1)
                dve.wait_ge(sx2_ready, b + 1)
                for dst, w, s_ready in ((xk2, "ffn_k", xk2_ready), (xr2, "ffn_r", xr2_ready)):
                    for s in range(SL):
                        v.scalar_tensor_tensor(dst[:, s, :], sx2[:, s, :], vecs[w][:, s:s + 1], xc[:, s, 1:ROW], ALU.mult, ALU.add)\
                            .then_inc(s_ready, 1)

            def back_out(b):
                dve.wait_ge(back_filled["fv"], b + 1)
                ps = halves(back0)
                dve.wait_ge(rr_ready, b + 1)
                v.scalar_tensor_tensor(o_sb, o_sb, 1.0, ps, ALU.add, ALU.mult).then_inc(gated_ffn, 1)
                dve.wait_ge(gated_ffn, b + 1)
                v.scalar_tensor_tensor(x_res[:, :, :], o_sb, 0.5, x_res[:, :, :], ALU.mult, ALU.add).then_inc(out_ready, 1)

            def phase_a(b, tail, nb):
                wkv_bonus(b)
                for c in range(AHEAD):
                    wkv_prod(b, c)
                if tail is not None: back_ln(tail)
                mix(b, MIX_G)
                wkv_bonus_v(b)
                if tail is not None: back_shift(tail)
                wkv_kv(b, AHEAD)
                mix_add(b, MIX_G)
                for c in range(AHEAD, NCH - BEHIND):
                    wkv_scan(b, c)
                    if nb is not None and c == 7: front_scores(nb)
                    if nb is not None and c == 11: front_ln(nb)
                    if nb is not None and c == 12: front_shift(nb)
                    if c == 12: front_gate(b)
                    wkv_kv(b, c + 1)
                    wkv_prod(b, c)
                    if tail is not None and c == 8: back_out(tail)
                    if nb is not None and c == 7: front_inverse(nb)
                if nb is not None:
                    mix(nb, MIX_V)
                    mix_add(nb, MIX_V)
                    mix(nb, MIX_W)
                    mix_add(nb, MIX_W)

            def phase_b(b, nb):
                if b is not None:
                    for c in range(NCH - BEHIND, NCH - 1):
                        wkv_scan(b, c)
                        wkv_kv(b, c + 1)
                        wkv_prod(b, c)
                    wkv_scan(b, NCH - 1)
                    wkv_prod(b, NCH - 1)
                if nb is not None:
                    mix(nb, MIX_K)
                    mix_add(nb, MIX_K)
                if b is not None:
                    wkv_finish(b)
                    back_centre(b)
                if nb is not None:
                    wkv_kv(nb, 0)
                    wkv_kv(nb, 1)
                    mix(nb, MIX_R)
                    mix_add(nb, MIX_R)
                    for c in range(2, AHEAD): wkv_kv(nb, c)
                if b is not None: back_scale(b)
                if nb is not None:
                    for c in range(AHEAD - 1): wkv_scan(nb, c)
                if b is not None: back_gate(b)
                if nb is not None: wkv_scan(nb, AHEAD - 1)

            v.memset(eps_col[:, :], EPS).then_inc(consts_set, 1)
            v.memset(half_neg[:, :], -0.5).then_inc(consts_set, 1)
            v.memset(decay[:, :, :, 0:1], 0.0).then_inc(consts_set, 1)
            dve.wait_ge(consts_set, 3)
            dve.wait_ge(w_l0, W_L0)
            front_scores(0)
            front_inverse(0)
            front_ln(0)
            dve.wait_ge(w_mix, W_MIX)
            front_shift(0)
            mix(0, MIX_V)
            mix_add(0, MIX_V)
            mix(0, MIX_W)
            mix_add(0, MIX_W)
            phase_b(None, 0)
            dve.wait_ge(w_back, W_BACK)
            phase_a(0, None, 1)
            phase_b(0, 1)
            with dve.Fori(1, B - 1) as b:
                phase_a(b, b - 1, b + 1)
                phase_b(b, b + 1)
            phase_a(B - 1, B - 2, None)
            phase_b(B - 1, None)
            back_ln(B - 1)
            back_shift(B - 1)
            back_out(B - 1)

        @block.scalar
        def _(act):
            a = nc.scalar.activation

            def front_qk(b):
                act.wait_ge(front_filled, filled(b, "qk"))
                ps = front_unit("qk")
                a(qk[:, 0, :], ps[0:DQ, 0:E], ACT.Identity, bias=bq[:, 0:1]).then_inc(qk_ready, 1)
                a(qk[:, 1, :], ps[DQ:2 * DQ, E:2 * E], ACT.Identity, bias=bk[:, 0:1]).then_inc(qk_ready, 1)

            def front_v0(b, tail):
                act.wait_ge(front_filled, filled(b, "v0"))
                ps = front_unit("v0")
                if tail is not None:
                    act.wait_ge(xr2_ready, (tail + 1) * SL)
                a(vT[:, :, :].rearrange("p m c -> p (m c)"), ps[:, :], ACT.Copy).then_inc(vT_ready, 1)

            def front_exp(b, tail):
                if tail is not None:
                    act.wait_ge(back_filled["fr"], tail + 1)
                for use, n0 in (("s01", 0), ("s23", 2)):
                    act.wait_ge(front_filled, filled(b, use))
                    ps = halves(front_unit(use))
                    for n in (n0, n0 + 1):
                        act.wait_ge(max_ready, b * NT + n + 1)
                        ins = a(attn[:, n, :], ps[:, n - n0, :], ACT.Exp, bias=score_max[:, n:n + 1], accum_out=row_sum[:, n:n + 1])
                        ins.then_inc(exp_ready, 1)

            def front_normalise(b):
                for n in range(NT):
                    act.wait_ge(inv_ready, b * NT + n + 1)
                    a(attn[:, n, :], attn[:, n, :], ACT.Copy, scale=row_inv[:, n:n + 1]).then_inc(attn_ready, 1)

            def front_attnT(b, tail):
                for use, m0 in (("t01", 0), ("t23", 2)):
                    if tail is not None and m0 == 0:
                        act.wait_ge(back_filled["fv"], tail + 1)
                    elif tail is not None:
                        act.wait_ge(out_ready, tail + 1)
                    act.wait_ge(front_filled, filled(b, use))
                    a(attnT[:, m0:m0 + 2, :], halves(front_unit(use)), ACT.Copy).then_inc(attnT_ready, 1)

            def front_xa(b):
                act.wait_ge(prev_att_landed, (b + 1) * 16 * G)
                if later(b):
                    act.wait_ge(xm_ready, b * NMIX)
                a(xa[:, :, 0], prev_att[:, :], ACT.Copy).then_inc(xa_ready, 1)
                act.wait_ge(front_filled, filled(b, "xnT"))
                ps = slots(front_unit("xnT"))
                for s in range(SL):
                    last = a(xa[:, s, 1:ROW], ps[:, s, :], ACT.Identity, bias=vecs["ln1_b"][:, s:s + 1], scale=vecs["ln1_w"][:, s:s + 1])
                    last.then_inc(xa_ready, 1)

            def front_h(b):
                act.wait_ge(front_filled, filled(b, "w1"))
                ps = front_unit("w1")
                a(h_a[:, :], ps[:, 0:TOK], ACT.Tanh).then_inc(h_ready, 1)
                a(h_b[:, :], ps[DD:DD + DM, E:E + TOK], ACT.Tanh).then_inc(h_ready, 1)

            def td_hidden(b):
                act.wait_ge(back_filled["td1"], b + 1)
                ps = back0
                a(tw[:, :], ps[0:DD, 0:TOK], ACT.Tanh).then_inc(tw_ready, 1)

            def td_out(b):
                act.wait_ge(front_filled, filled(b, "td2"))
                ps = slots(front_unit("td2"))
                if later(b):
                    act.wait_ge(reduced, b * SL)
                for s in range(SL):
                    a(rate[:, s, :], ps[:, s, :], ACT.Exp, bias=vecs["time_decay"][:, s:s + 1]).then_inc(rate_ready, 1)
                act.wait_ge(rate_ready, (b + 1) * SL)
                if later(b):
                    act.wait_ge(scanned, b * 2 * NCH)
                for s in range(SL):
                    a(decay[:, s, :, 1:ROW], rate[:, s, :].unsqueeze(1).to_broadcast([P, 2, TOK]), ACT.Exp, scale=-1.0).then_inc(decay_ready, 1)

            def evacuate(b, use, dst, ready, former, per):
                act.wait_ge(front_filled, filled(b, use))
                ps = front_unit(use)
                if later(b):
                    act.wait_ge(former, b * per)
                a(dst.rearrange("p s t -> p (s t)"), ps[:, :], ACT.Copy).then_inc(ready, 1)

            def front_th(b):
                act.wait_ge(back_filled["g"], b + 1)
                ps = back0
                if later(b):
                    act.wait_ge(gated, b)
                a(gate[:, :, :].rearrange("p s t -> p (s t)"), ps[:, :], ACT.Tanh, scale=0.5).then_inc(th_ready, 1)

            def save_residual(b):
                act.wait_ge(x_mid_ready, (b + 1) * CT)
                if later(b):
                    act.wait_ge(out_stored, b * 16)
                a(x_res[:, :, :], x_mid[:, :, :], ACT.Copy).then_inc(res_ready, 1)

            def wkv_row0(b, c):
                s, g = divmod(c, G)
                if c == 0:
                    act.wait_ge(state_landed, (b + 1) * 16 * G)
                    if later(b):
                        act.wait_ge(reduced, b * SL)
                elif c == 2:
                    act.wait_ge(front_filled, filled(b, "k"))
                    act.wait_ge(back_filled["td1"], b + 1)
                elif c == 5:
                    act.wait_ge(front_filled, filled(b, "r"))
                elif c == 6:
                    act.wait_ge(decay_ready, (b + 1) * SL)
                if c >= NS:
                    act.wait_ge(reduced, b * SL + (c - NS) // G + 1)
                a(states[:, buf(c), :, 0], state0[:, s * D + g * SL:s * D + (g + 1) * SL], ACT.Copy).then_inc(row0_ready, 1)

            def back_square(b):
                act.wait_ge(centred, b + 1)
                a(sq[:, :, :], y[:, :, :], ACT.Square).then_inc(sq_ready, 1)

            def back_gvar(b):
                act.wait_ge(back_filled["var"], b + 1)
                ps = back1
                a(rstd[:, :], ps[:, 0:TOK], ACT.Sqrt, bias=eps_col[:, 0:1]).then_inc(gvar_ready, 1)

            def back_affine(b):
                act.wait_ge(normed, b + 1)
                for s in range(SL):
                    a(y[:, s, :], y[:, s, :], ACT.Identity, bias=vecs["gn_b"][:, s:s + 1], scale=vecs["gn_w"][:, s:s + 1]).then_inc(affine, 1)

            def back_xc(b):
                act.wait_ge(prev_ffn_landed, (b + 1) * 16 * G)
                a(xc[:, :, 0], prev_ffn[:, :], ACT.Copy).then_inc(xc_ready, 1)
                act.wait_ge(back_filled["xcT"], b + 1)
                ps = slots(back1)
                for s in range(SL):
                    a(xc[:, s, 1:ROW], ps[:, s, :], ACT.Identity, bias=vecs["ln2_b"][:, s:s + 1], scale=vecs["ln2_w"][:, s:s + 1]).then_inc(xc_ready, 1)

            def back_kk(b):
                act.wait_ge(back_filled["fk"], b + 1)
                ps = slots(back0)
                a(kk, ps, ACT.Relu).then_inc(relu_ready, 1)
                act.wait_ge(relu_ready, b + 1)
                a(kk, kk, ACT.Square).then_inc(kk_ready, 1)

            def back_rr(b):
                act.wait_ge(back_filled["fr"], b + 1)
                ps = halves(back0)
                a(o_sb, ps, ACT.Tanh, scale=0.5).then_inc(rr_ready, 1)

            def phase_a(b, tail, nb):
                if nb is not None: front_qk(nb)
                for c in range(AHEAD, NS):
                    wkv_row0(b, c)
                if tail is not None: back_xc(tail)
                if nb is not None: front_v0(nb, tail)
                if tail is not None: back_kk(tail)
                for c in range(NS, G + NS):
                    wkv_row0(b, c)
                if tail is not None: back_rr(tail)
                if nb is not None:
                    front_exp(nb, tail)
                    front_normalise(nb)
                    front_attnT(nb, tail)
                save_residual(b)
                for c in range(G + NS, NCH - 1):
                    wkv_row0(b, c)
                if nb is not None: front_xa(nb)
                front_th(b)
                wkv_row0(b, NCH - 1)
                if nb is not None: front_h(nb)

            def phase_b(b, nb):
                if nb is not None:
                    evacuate(nb, "v", v_sb[:, :, :], v_ready, bonus_v_ready, 1)
                    td_hidden(nb)
                if b is not None: back_square(b)
                if nb is not None:
                    evacuate(nb, "k", k_sb[:, :, :], k_ready, kv_ready, NCH)
                    td_out(nb)
                    for c in range(AHEAD): wkv_row0(nb, c)
                if b is not None:
                    back_gvar(b)
                    back_affine(b)
                if nb is not None: evacuate(nb, "r", r_sb[:, :, :], r_ready, prod_ready, NCH)

            act.wait_ge(consts_set, 3)
            act.wait_ge(w_qk, W_QK)
            front_qk(0)
            front_v0(0, None)
            front_exp(0, None)
            front_normalise(0)
            front_attnT(0, None)
            act.wait_ge(w_mix, W_MIX)
            front_xa(0)
            front_h(0)
            phase_b(None, 0)
            act.wait_ge(w_back, W_BACK)
            phase_a(0, None, 1)
            phase_b(0, 1)
            with act.Fori(1, B - 1) as b:
                phase_a(b, b - 1, b + 1)
                phase_b(b, b + 1)
            phase_a(B - 1, B - 2, None)
            phase_b(B - 1, None)
            back_xc(B - 1)
            back_kk(B - 1)
            back_rr(B - 1)

        @block.gpsimd
        def _(pool):
            g_ = nc.gpsimd

            def ln_power(b, lvar_s, lrstd_s):
                pool.wait_ge(lvar_s, b + 1)
                g_.tensor_tensor(ln_rstd[:, :], ln_var[:, :], half_neg[:, 0:1].to_broadcast([P, CT]), ALU.pow).then_inc(lrstd_s, 1)

            def phase_a(tail, nb):
                if tail is not None: ln_power(tail, lvar2_ready, lrstd2_ready)
                if nb is not None: ln_power(nb, lvar_ready, lrstd_ready)

            pool.wait_ge(consts_set, 3)
            ln_power(0, lvar_ready, lrstd_ready)
            phase_a(None, 1)
            with pool.Fori(1, B - 1) as b:
                phase_a(b - 1, b + 1)
            phase_a(B - 2, None)
            phase_a(B - 1, None)


def kernel(**inputs):
    import numpy as np
    import concourse.bacc as bacc
    from concourse import mybir as _mybir
    from concourse.bass_utils import run_bass_kernel_spmd as run

    def t(name):
        return np.asarray(inputs[name])

    def channels(w, axis):
        shape = w.shape
        w = w.reshape(shape[:axis] + (H, G, SL) + shape[axis + 1:]).swapaxes(axis, axis + 1)
        return w.reshape(shape[:axis] + (P, SL) + shape[axis + 1:])

    def proj(name):
        return channels(channels(t(name).T, 1), 0).swapaxes(2, 3)

    pre0, pre1 = "L0_xattn_", "L1_xattn_"
    part = np.arange(P)
    same_head = (part[:, None] % H == part[None, :] % H).astype(np.float32)
    arrays = {
        "x": t("x"), "ctx": t("ctx_2048"),
        "wq": t(pre0 + "Wq").T.reshape(CT, P, DQ).transpose(1, 0, 2),
        "wk": t(pre0 + "Wk").T.reshape(CT, P, DQ).transpose(1, 0, 2),
        "wv": t(pre0 + "Wv").T.reshape(CT, P, TOK).transpose(1, 0, 2),
        "bq": t(pre0 + "bq").reshape(DQ, 1), "bk": t(pre0 + "bk").reshape(DQ, 1),
        "bv": t(pre0 + "bv").reshape(CT, P).T,
        "ident": np.eye(P, dtype=np.float32), "red": same_head[:, 0:H],
        "head_sum": same_head, "head_mean": same_head * np.float32(1.0 / D),
        "maa_stack": channels(t(pre1 + "maa_stack").reshape(NMIX, E), 1).transpose(1, 0, 2),
        "maa_w1": channels(t(pre1 + "maa_w1"), 0),
        "maa_w2": channels(t(pre1 + "maa_w2").reshape(NMIX * DM, E), 1).transpose(0, 2, 1),
        "td_w1": channels(t(pre1 + "td_w1"), 0),
        "td_w2": channels(t(pre1 + "td_w2"), 1).transpose(0, 2, 1),
        "ffn_k": channels(t(pre1 + "ffn_maa_k"), 0), "ffn_r": channels(t(pre1 + "ffn_maa_r"), 0),
        "Wo": channels(t(pre1 + "Wo").T, 0), "Wfr": channels(t(pre1 + "Wfr").T, 0), "Wfv": channels(t(pre1 + "Wfv").T, 0),
    }
    for n in ["ln1_w", "ln1_b", "maa_x", "time_decay", "u", "gn_w", "gn_b", "ln2_w", "ln2_b"]:
        arrays[n] = channels(t(pre1 + n).reshape(E), 0)
    for n in ["Wr", "Wk", "Wv", "Wg", "Wfk"]:
        arrays[n] = proj(pre1 + n)

    nc = bacc.Bacc("TRN2", target_bir_lowering=False, num_devices=1)
    io, given = {}, {}
    for n in _INS:
        arr = np.ascontiguousarray(arrays[n])
        given[f"in_{n}"] = arr
        io[n] = nc.dram_tensor(f"in_{n}", arr.shape, _mybir.dt.from_np(arr.dtype), kind="ExternalInput").ap()
    out = nc.dram_tensor("out", (B, TOK, E), _mybir.dt.float32, kind="ExternalOutput").ap()
    xattn_rwkv_kernel(nc, io, out)
    result = run(nc, [given], core_ids=[0])
    return result.results[0]["out"]
```
